# Optimizing a Trainium2 kernel written in Bass

```python
import numpy as np
import jax
import jax.numpy as jnp

def _softmax(x, axis=-1):
    return jax.nn.softmax(x, axis=axis)

def _gelu(x):
    return jax.nn.gelu(x, approximate=True)

def _silu(x):
    return jax.nn.silu(x)

def _sigmoid(x):
    return jax.nn.sigmoid(x)

def _layernorm(x, axis=-1, eps=1e-05):
    m = jnp.mean(x, axis=axis, keepdims=True)
    v = jnp.var(x, axis=axis, keepdims=True)
    return (x - m) / jnp.sqrt(v + eps)

def _scatter_add(tgt, idx, src, axis=0):
    return tgt.at[idx].add(src)

def _segment_sum(src, seg, n):
    return jax.ops.segment_sum(src, seg, n)
kernel_name = 'mk_adj_ffn_d1_adj_r2_2a3826'

def setup_inputs(seed: int=0):
    np.random.seed(seed)
    _w = jnp.asarray

    def _rec_inputs():
        import jax
        import jax.numpy as jnp
        _gk = jax.random.key(seed)
        x = -0.0002928 + 1 * jax.random.normal(jax.random.fold_in(_gk, 1), (64, 128, 128), jnp.float32)
        _a = jax.random.bernoulli(jax.random.fold_in(_gk, 2), 0.03125, (64, 128, 128))
        _a = jnp.logical_or(_a, jnp.swapaxes(_a, -1, -2))
        _a = jnp.logical_or(_a, jnp.eye(128, dtype=bool))
        adj = _a.astype(jnp.int32)
        return (x, adj)
    x, adj = _rec_inputs()

    def _L0_gnn_setup():
        import jax, jax.numpy as jnp
        import numpy as np
        key = jax.random.key(seed)
        k1, k2, k3, k4 = jax.random.split(key, 4)
        B, N, F, U = (8, 1024, 128, 128)
        x = jax.random.normal(k1, (B, N, F), dtype=jnp.float32)
        adj = jax.random.randint(k2, (B, N, N), 0, 2, dtype=jnp.int32)
        W_msg = jax.random.normal(k3, (F, U), dtype=jnp.float32) / np.sqrt(F)
        W_upd = jax.random.normal(k4, (F, U), dtype=jnp.float32) / np.sqrt(F)
        bias = jnp.zeros((U,), dtype=jnp.float32)
        return {'x': x, 'adj': adj, 'W_msg': W_msg, 'W_upd': W_upd, 'bias': bias}
    _L0_gnn_all = _L0_gnn_setup()
    _L0_gnn_in = {k: v for k, v in _L0_gnn_all.items() if k in ('W_msg', 'W_upd', 'bias')}
    del _L0_gnn_all

    def _L0_ffn_setup():
        import jax, jax.numpy as jnp
        import numpy as np
        TOP_K = 2
        LN_EPS = 1e-05
        key = jax.random.key(seed)
        ks = jax.random.split(key, 8)
        B, S, D, E, H = (16, 512, 128, 8, 512)
        x = jax.random.normal(ks[0], (B, S, D), dtype=jnp.float32)
        Wr = jax.random.normal(ks[1], (D, E), dtype=jnp.float32) * 0.1
        br = jnp.zeros((E,), dtype=jnp.float32)
        ln_g = jnp.ones((E, D), dtype=jnp.float32)
        ln_b = jnp.zeros((E, D), dtype=jnp.float32)
        W1 = jax.random.normal(ks[2], (E, D, H), dtype=jnp.float32) * (1.0 / np.sqrt(D))
        b1 = jnp.zeros((E, H), dtype=jnp.float32)
        W2 = jax.random.normal(ks[3], (E, H, D), dtype=jnp.float32) * (1.0 / np.sqrt(H))
        b2 = jnp.zeros((E, D), dtype=jnp.float32)
        return {'x': x, 'Wr': Wr, 'br': br, 'ln_g': ln_g, 'ln_b': ln_b, 'W1': W1, 'b1': b1, 'W2': W2, 'b2': b2}
    _L0_ffn_all = _L0_ffn_setup()
    _L0_ffn_in = {k: v for k, v in _L0_ffn_all.items() if k in ('Wr', 'br', 'ln_g', 'ln_b', 'W1', 'b1', 'W2', 'b2')}
    del _L0_ffn_all
    return {'x': x, 'adj': adj, 'L0_gnn_W_msg': _L0_gnn_in['W_msg'], 'L0_gnn_W_upd': _L0_gnn_in['W_upd'], 'L0_gnn_bias': _L0_gnn_in['bias'], 'L0_ffn_Wr': _L0_ffn_in['Wr'], 'L0_ffn_br': _L0_ffn_in['br'], 'L0_ffn_ln_g': _L0_ffn_in['ln_g'], 'L0_ffn_ln_b': _L0_ffn_in['ln_b'], 'L0_ffn_W1': _L0_ffn_in['W1'], 'L0_ffn_b1': _L0_ffn_in['b1'], 'L0_ffn_W2': _L0_ffn_in['W2'], 'L0_ffn_b2': _L0_ffn_in['b2']}

def reference(x, adj, L0_gnn_W_msg, L0_gnn_W_upd, L0_gnn_bias, L0_ffn_Wr, L0_ffn_br, L0_ffn_ln_g, L0_ffn_ln_b, L0_ffn_W1, L0_ffn_b1, L0_ffn_W2, L0_ffn_b2):
    import jax
    import jax.numpy as jnp

    def _L0_gnn_ref(x, adj, W_msg, W_upd, bias):
        import jax, jax.numpy as jnp
        import numpy as np
        a = adj.astype(x.dtype)
        h = jnp.einsum('bnf,fu->bnu', x, W_msg)
        msg_sum = jnp.einsum('bij,biu->bju', a, h)
        deg = jnp.sum(a, axis=1)
        messages = jnp.where(deg[..., None] > 0, msg_sum / jnp.maximum(deg, 1.0)[..., None], 0.0)
        out = jnp.einsum('bnf,fu->bnu', x, W_upd) + messages + bias
        return jax.nn.relu(out)

    def _L0_ffn_ref(x, Wr, br, ln_g, ln_b, W1, b1, W2, b2):
        import jax, jax.numpy as jnp
        import numpy as np
        TOP_K = 2
        LN_EPS = 1e-05
        B, S, D = x.shape
        N = B * S
        xt = x.reshape(N, D)
        logits = xt @ Wr + br
        probs = jax.nn.softmax(logits, axis=-1)
        top_p, top_idx = jax.lax.top_k(probs, TOP_K)
        weights = top_p / top_p.sum(axis=-1, keepdims=True)
        mu = xt.mean(axis=-1, keepdims=True)
        var = ((xt - mu) ** 2).mean(axis=-1, keepdims=True)
        xn = (xt - mu) * jax.lax.rsqrt(var + LN_EPS)
        xe = xn[None, :, :] * ln_g[:, None, :] + ln_b[:, None, :]
        h = jax.nn.gelu(jnp.einsum('end,edh->enh', xe, W1) + b1[:, None, :], approximate=False)
        y = jnp.einsum('enh,ehd->end', h, W2) + b2[:, None, :]
        y_tok = jnp.transpose(y, (1, 0, 2))
        sel = jnp.take_along_axis(y_tok, top_idx[:, :, None], axis=1)
        out = (weights[:, :, None] * sel).sum(axis=1)
        return out.reshape(B, S, D)
    x = x + _L0_gnn_ref(_layernorm(x, axis=-1), adj, L0_gnn_W_msg, L0_gnn_W_upd, L0_gnn_bias)
    x = x + _L0_ffn_ref(_layernorm(x, axis=-1), L0_ffn_Wr, L0_ffn_br, L0_ffn_ln_g, L0_ffn_ln_b, L0_ffn_W1, L0_ffn_b1, L0_ffn_W2, L0_ffn_b2)
    return x

_drawn_inputs = setup_inputs


def setup_inputs(seed=0):
    import zlib

    import numpy as np

    out = dict(_drawn_inputs(seed))
    spreads = {'L0_gnn_bias': (0.0, 0.1),
     'L0_ffn_br': (0.0, 0.1),
     'L0_ffn_ln_g': (1.0, 0.2),
     'L0_ffn_ln_b': (0.0, 0.1),
     'L0_ffn_b1': (0.0, 0.1),
     'L0_ffn_b2': (0.0, 0.1)}
    factors = {}
    for name, (base, spread) in spreads.items():
        noise = np.random.default_rng([zlib.crc32(name.encode()), seed]).standard_normal(out[name].shape)
        drawn = base * np.exp(spread * noise) if base else spread * noise
        out[name] = jnp.asarray(drawn.astype(out[name].dtype))
    for name, factor in factors.items():
        out[name] = (out[name] * factor).astype(out[name].dtype)
    return out
```

```python
import numpy as np
import concourse.bass as bass
from concourse import mybir
from contextlib import ExitStack

F32, F16, BF16, I32 = mybir.dt.float32, mybir.dt.float16, mybir.dt.bfloat16, mybir.dt.int32
ALU = mybir.AluOpType
ACT = mybir.ActivationFunctionType
AX = mybir.AxisListType

P = 128
B, N, D = 64, 128, 128
E, H = 8, 512
C = H // P
TOKENS = B * N
EPS = 1e-5

G = 8
HG = G // 2
STEPS = B // G

PAIRS = [(a, b) for a in range(E) for b in range(a + 1, E)]
NP = len(PAIRS)
SEG = TOKENS + P
PAD_SEG = NP * SEG
TILES = TOKENS // P + NP - 1

MU, RS, WA, WB, TOK, ROW = D, D + 1, D + 2, D + 3, D + 4, D + 8

BIG = -3.0e38


class Done:

    def __init__(self, engine, sem):
        self.engine, self.sem, self.base, self.n = engine, sem, 0, 0

    def __call__(self, instruction):
        instruction.then_inc(self.sem, 1)
        self.n += 1
        return self.base + self.n

    def wait(self, mark):
        self.engine.wait_ge(self.sem, mark)

    def rebase(self, base):
        self.base, self.n = base, 0


def moe_gnn(nc, x, adj, W_msg, W_upd, bias, Wr, br, ln_g, ln_b, W1, b1, W2, b2, out):
    ctx = ExitStack()
    with ctx:
        def sb(name, shape, dt):
            return ctx.enter_context(nc.sbuf_tensor(name, shape, dt))

        def sem(name):
            return ctx.enter_context(nc.semaphore(name))

        rows = nc.dram_tensor("rows", (PAD_SEG + P, ROW), F32, kind="Internal").ap()

        ident = sb("ident", [P, P], F32)
        ones_f = sb("ones_f", [P, 1], F32)
        ones_row = sb("ones_row", [1, P], F32)
        tri = sb("tri", [P, P], BF16)
        ones_b = sb("ones_b", [P, P], BF16)
        rev = sb("rev", [P, G, E], F32)
        keys = sb("keys", [P, G, NP], F32)
        rowb = sb("rowb", [P, G, NP], F32)
        exp_a = sb("exp_a", [P, NP], F32)
        exp_b = sb("exp_b", [P, NP], F32)
        tcol = sb("tcol", [P, 1], F32)
        tok = sb("tok", [P, G], F32)
        nhalf = sb("nhalf", [P, 2 * G], F32)
        padrow = sb("padrow", [P, ROW], F32)

        wmsg = sb("wmsg", [P, D], F32)
        wupd = sb("wupd", [P, D], F32)
        wr = sb("wr", [P, E], F32)
        brb = sb("brb", [P, E], F32)
        bias_row = sb("bias_row", [1, HG, D], F32)
        w1f = sb("w1f", [P, E, H], F32)
        w2f = sb("w2f", [P, E, C, D], F32)
        w1h = sb("w1h", [P, E, C, P], F16)
        w1l = sb("w1l", [P, E, C, P], F16)
        w2h = sb("w2h", [P, E, C, D], F16)
        w2l = sb("w2l", [P, E, C, D], F16)
        small_rows = sb("small_rows", [2 * E + E * C, P], F32)
        small_cols = sb("small_cols", [P, 2 * E + E * C], F32)
        b2row = sb("b2row", [2, E, D], F32)
        b2sc = sb("b2sc", [2, E, D], F32)
        b2hi = sb("b2hi", [2, E, D], F16)
        b2t = sb("b2t", [P, E, D], F16)
        b2hi32 = sb("b2hi32", [2, E, D], F32)
        halfsel = sb("halfsel", [2, 1], F32)
        ones2 = sb("ones2", [P, P], F16)
        b1s = sb("b1s", [P, E * C], F32)
        gsc = sb("gsc", [P, E], F32)
        amax = sb("amax", [P, 4], F32)
        amax_all = sb("amax_all", [P, 4], F32)
        amw = sb("amw", [P, E], F32)
        sc = sb("sc", [P, 16], F32)

        X = sb("X", [P, 2, G, D], F32)
        ADJ = sb("ADJ", [P, 2, G, N], I32)
        AF = sb("AF", [P, G, N], F32)
        XN = sb("XN", [P, G, D], F32)
        XNT = sb("XNT", [P, 2, HG * P], F32)
        AGT = sb("AGT", [P, 2, HG * P], F32)
        U = sb("U", [P, 2, HG, D], F32)
        T = sb("T", [P, 2, HG, D], F32)
        SR = sb("SR", [P, 2, G, ROW], F32)
        XT = sb("XT", [P, G, D], F32)
        XTT = sb("XTT", [P, 2, HG * P], F32)
        st1 = sb("st1", [P, G, 6], F32)
        mv1 = sb("mv1", [P, G, 2], F32)
        ve1 = sb("ve1", [P, G], F32)
        r1 = sb("r1", [P, G], F32)
        st2 = sb("st2", [P, G, 6], F32)
        mv2 = sb("mv2", [P, G, 2], F32)
        ve2 = sb("ve2", [P, 2, G], F32)
        r2 = sb("r2", [P, 2, G], F32)
        dg = sb("dg", [P, 3, G], F32)
        L = sb("L", [P, 4, G, E], F32)
        rt = sb("rt", [P, 20, G], F32)
        oh = sb("oh", [P, G, NP], BF16)
        pre = sb("pre", [P, G + 1, NP], BF16)
        rk = sb("rk", [P, G, NP], F32)
        pos = sb("pos", [P, 2, G], I32)

        cntf = sb("cntf", [P, NP], F32)
        cnti = sb("cnti", [P, NP], I32)
        ntf = sb("ntf", [P, NP], F32)
        inc = sb("inc", [P, 2, NP], F32)
        tw = sb("tw", [P, 4, NP], F32)
        fld = sb("fld", [P, 4], F32)
        tab = sb("tab", [1, 3, P], I32)
        fill = sb("fill", [1, NP], I32)

        RA = sb("RA", [P, 4, ROW], F32)
        RC = sb("RC", [P, 4, ROW], F32)
        xs = sb("xs", [P, 2, D], F32)
        xh = sb("xh", [P, 2, P], F16)
        xl = sb("xl", [P, 2, P], F16)
        gl = sb("gl", [P, 4, H], F32)
        hh = sb("hh", [P, 4, H], F16)
        hl = sb("hl", [P, 4, H], F16)
        o = sb("o", [P, 4, D], F32)
        o1 = sb("o1", [P, 2, D], F32)

        bank = [ctx.enter_context(nc.psum_tensor(f"bank{i}", [P, 512], F32)) for i in range(8)]

        consts = sem("consts")
        gnn_w = sem("gnn_w")
        ffn_w = sem("ffn_w")
        x_in = [sem(f"x_in{i}") for i in range(2)]
        adj_in = [sem(f"adj_in{i}") for i in range(2)]
        dve = sem("dve_done")
        setup_pe = sem("setup_pe")
        amax_in = sem("amax_in")
        amax_out = sem("amax_out")
        ve1_ready, r1_ready = sem("ve1_ready"), sem("r1_ready")
        ve2_ready, r2_ready = sem("ve2_ready"), sem("r2_ready")
        xn_ready, xt_ready = sem("xn_ready"), sem("xt_ready")
        ta_done, s2_done, xt_done, lg_done = sem("ta_done"), sem("s2_done"), sem("xtr_done"), sem("lg_done")
        adj_f32 = sem("adj_f32")
        xnt_ready, u_ready, xtt_ready = sem("xnt_ready"), sem("u_ready"), sem("xtt_ready")
        deg_used, msg_used, x2_ready = sem("deg_used"), sem("msg_used"), sem("x2_ready")
        lg_used, gap_ready, ex_ready = sem("lg_used"), sem("gap_ready"), sem("ex_ready")
        oh_ready, rank_done, pos_ready = sem("oh_ready"), sem("rank_done"), sem("pos_ready")
        rows_free = sem("rows_free")
        scattered = [sem(f"scattered{i}") for i in range(2)]
        total_done, fld_ready, fld_row = sem("total_done"), sem("fld_ready"), sem("fld_row")
        tab_ready, fill_ready, padded = sem("tab_ready"), sem("fill_ready"), sem("padded")
        weights_ready = sem("weights_ready")
        ra_in = [sem(f"ra_in{i}") for i in range(4)]
        rc_in = [sem(f"rc_in{i}") for i in range(4)]
        xs_ready, xtb_done, xh_ready, xl_ready = sem("xs_ready"), sem("xtb_done"), sem("xh_ready"), sem("xl_ready")
        z_done, g_ready, h_ready, y_done = sem("z_done"), sem("g_ready"), sem("h_ready"), sem("y_done")
        o_ready = sem("o_ready")
        passed = sem("passed")
        stored = [sem(f"stored{i}") for i in range(4)]

        block = ctx.enter_context(nc.Block())

        N_GNN_W = 5 + HG
        N_FFN_W = 6

        def wait_alone(eng, semaphore, value):
            eng.wait_ge(semaphore, value)
            eng.sem_inc(passed, 1)

        def live(j, lag, n):
            return not isinstance(j, int) or 0 <= j - lag < n

        def late(j, k):
            return not isinstance(j, int) or j - k >= 0

        def stage_a(eng, step, rebase=None):
            step(0, 0, 0)
            step(1, 0, 1)
            with eng.Fori(1, STEPS // 2) as i:
                if rebase:
                    rebase(i)
                step(2 * i, i, 0)
                step(2 * i + 1, i, 1)
            if rebase:
                rebase(STEPS // 2)
            step(STEPS, STEPS // 2, 0)
            step(STEPS + 1, STEPS // 2, 1)

        B_FIRST = 4
        B_TURNS = (TILES - 3 - B_FIRST) // 4
        B_LAST = B_FIRST + 4 * B_TURNS

        def stage_b(eng, step, last, rebase=None):
            for t in range(B_FIRST):
                step(t, t // 4, t % 4)
            with eng.Fori(1, 1 + B_TURNS) as i:
                if rebase:
                    rebase(i)
                for k in range(4):
                    step(4 * i + k, i, k)
            if rebase:
                rebase(1 + B_TURNS)
            for t in range(B_LAST, last):
                step(t, t // 4, t % 4)

        @block.sync
        def _(sp):
            def load(j, jh, par):
                if not live(j, 0, STEPS):
                    return
                if late(j, 2):
                    wait_alone(sp, x2_ready, 2 * (j - 1))
                    wait_alone(sp, adj_f32, j - 1)
                sp.dma_start(X[:, par], x[bass.ds(j * G, G)].rearrange("g n f -> n g f"))\
                    .then_inc(x_in[par], 16)
                sp.dma_start(ADJ[:, par], adj[bass.ds(j * G, G)].rearrange("g n f -> n g f"))\
                    .then_inc(adj_in[par], 16)

            load(0, 0, 0)
            load(1, 0, 1)
            with sp.Fori(1, STEPS // 2) as i:
                load(2 * i, i, 0)
                load(2 * i + 1, i, 1)

            sp.wait_ge(consts, N_CONSTS)
            sp.dma_start(rows[PAD_SEG:PAD_SEG + P, :], padrow[:, :]).then_inc(padded, 16)
            sp.wait_ge(fill_ready, 1)
            with sp.Fori(0, NP) as i:
                at = sp.value_load(fill[0:1, bass.ds(i, 1)], min_val=0, max_val=PAD_SEG - P)
                sp.dma_start(rows[bass.ds(at, P), :], padrow[:, :]).then_inc(padded, 16)
            for par in range(2):
                sp.wait_ge(scattered[par], 16 * G * STEPS // 2)
            sp.wait_ge(padded, 16 * (NP + 1))
            sp.wait_ge(tab_ready, 1)

            def tile_loads(t, th, q):
                if live(t, 0, TILES):
                    at = sp.value_load(tab[0:1, 2, bass.ds(t, 1)], min_val=0, max_val=PAD_SEG)
                    if late(t, 4):
                        wait_alone(sp, xs_ready, t - 3)
                    sp.dma_start(RA[:, q], rows[bass.ds(at, P), :]).then_inc(ra_in[q], 16)
                    if late(t, 4):
                        wait_alone(sp, o_ready, t - 3)
                        wait_alone(sp, stored[q], 16 * th)
                    sp.dma_start(RC[:, q], rows[bass.ds(at, P), :]).then_inc(rc_in[q], 16)

            stage_b(sp, tile_loads, TILES)
            for q in range(4):
                sp.wait_ge(stored[q], 16 * len(range(q, TILES, 4)))

        @block.gpsimd
        def _(pool):
            n = [0]

            def const(instruction):
                instruction.then_inc(consts, 1)
                n[0] += 1

            def settle():
                pool.wait_ge(consts, n[0])

            const(pool.memset(ident[:], 0.0))
            const(pool.memset(ones_f[:], 1.0))
            const(pool.memset(ones_row[:], 1.0))
            const(pool.memset(tri[:], 1.0))
            const(pool.memset(ones_b[:], 1.0))
            const(pool.memset(nhalf[:], -0.5))
            const(pool.memset(padrow[:], 0.0))
            const(pool.memset(pre[:], 0.0))
            const(pool.memset(SR[:], 0.0))
            const(pool.memset(b2t[:], 0.0))
            const(pool.memset(ones2[:], 0.0))
            const(pool.memset(amax[:], 0.0))
            settle()
            const(pool.affine_select(out=ident[:], in_=ident[:], compare_op=ALU.not_equal, fill=1.0, base=0,
                                     pattern=[[-1, P]], channel_multiplier=1))
            const(pool.affine_select(out=tri[:], in_=tri[:], compare_op=ALU.is_ge, fill=0.0, base=-1,
                                     pattern=[[1, P]], channel_multiplier=-1))
            const(pool.iota(rev[:], pattern=[[0, G], [-1, E]], base=E, channel_multiplier=0,
                            allow_small_or_imprecise_dtypes=True))
            off = 0
            for a in range(E - 1):
                k = E - 1 - a
                const(pool.iota(keys[:, :, off:off + k], pattern=[[0, G], [-1, k]],
                                base=E * (E - a) + E - (a + 1), channel_multiplier=0,
                                allow_small_or_imprecise_dtypes=True))
                const(pool.iota(exp_a[:, off:off + k], pattern=[[0, k]], base=a, channel_multiplier=0,
                                allow_small_or_imprecise_dtypes=True))
                const(pool.iota(exp_b[:, off:off + k], pattern=[[1, k]], base=a + 1, channel_multiplier=0,
                                allow_small_or_imprecise_dtypes=True))
                off += k
            const(pool.iota(rowb[:], pattern=[[0, G], [SEG, NP]], base=0, channel_multiplier=0,
                            allow_small_or_imprecise_dtypes=True))
            const(pool.iota(tcol[:], pattern=[[0, 1]], base=0, channel_multiplier=1,
                            allow_small_or_imprecise_dtypes=True))
            const(pool.iota(halfsel[:], pattern=[[0, 1]], base=0, channel_multiplier=1,
                            allow_small_or_imprecise_dtypes=True))
            const(pool.iota(tok[:], pattern=[[P, G]], base=0, channel_multiplier=1,
                            allow_small_or_imprecise_dtypes=True))
            const(pool.iota(padrow[:, TOK:TOK + 1].bitcast(I32), pattern=[[0, 1]], base=TOKENS,
                            channel_multiplier=0))
            assert n[0] == N_CONSTS, n[0]
            pool.sem_inc(rows_free, 1)

            pool.wait_ge(amax_in, 1)
            pool.partition_all_reduce(amax_all[:], amax[:], P, RMAX).then_inc(amax_out, 1)

            def step(j, jh, par):
                if live(j, 0, STEPS):
                    pool.wait_ge(ve1_ready, j + 1)
                    if late(j, 1):
                        pool.wait_ge(xn_ready, G * j)
                    pool.tensor_tensor(r1[:], ve1[:], nhalf[:, 0:G], ALU.pow).then_inc(r1_ready, 1)
                if live(j, 1, STEPS):
                    pool.wait_ge(ve2_ready, j)
                    if late(j, 2):
                        pool.wait_ge(xt_ready, (G + 1) * (j - 1))
                    pool.tensor_tensor(r2[:].rearrange("p a g -> p (a g)"), ve2[:].rearrange("p a g -> p (a g)"),
                                       nhalf[:], ALU.pow).then_inc(r2_ready, 1)
                if live(j, 2, STEPS):
                    wait_alone(pool, pos_ready, j - 1)
                    for g in range(G):
                        pool.indirect_dma_start(rows[:, :], bass.IndirectOffsetOnAxis(ap=pos[:, par, g:g + 1], axis=0),
                                                SR[:, par, g, :], None).then_inc(scattered[par], 16)
                    pool.wait_ge(scattered[par], 16 * G * jh)
                    pool.sem_inc(rows_free, 1)

            stage_a(pool, step)

            def store(t, th, q):
                if live(t, 0, TILES):
                    wait_alone(pool, o_ready, t + 1)
                    pool.indirect_dma_start(
                        out[:, :], bass.IndirectOffsetOnAxis(ap=RC[:, q, TOK:TOK + 1].bitcast(I32), axis=0),
                        o[:, q, :], None, bounds_check=TOKENS - 1, oob_is_err=False).then_inc(stored[q], 16)

            stage_b(pool, store, TILES)

        @block.scalar
        def _(act):
            act.dma_start(wmsg[:], W_msg).then_inc(gnn_w, 16)
            act.dma_start(wupd[:], W_upd).then_inc(gnn_w, 16)
            act.dma_start(wr[:], Wr).then_inc(gnn_w, 16)
            act.dma_start(brb[:], br.rearrange("(o e) -> o e", o=1).partition_broadcast(P)).then_inc(gnn_w, 16)
            act.dma_start(b2row[:], b2.rearrange("(o e) d -> o e d", o=1).partition_broadcast(2)).then_inc(gnn_w, 16)
            for g in range(HG):
                act.dma_start(bias_row[:, g, :], bias.rearrange("(o d) -> o d", o=1)).then_inc(gnn_w, 16)
            act.dma_start(small_rows[0:E, :], ln_g).then_inc(ffn_w, 16)
            act.dma_start(small_rows[E:2 * E, :], ln_b).then_inc(ffn_w, 16)
            act.dma_start(small_rows[2 * E:, :], b1.rearrange("e (c p) -> (e c) p", p=P)).then_inc(ffn_w, 16)
            act.dma_start(w1f[:], W1.rearrange("e d h -> d e h")).then_inc(ffn_w, 16)
            for e in range(2):
                act.dma_start(w2f[:, e * 4:(e + 1) * 4], W2[e * 4:(e + 1) * 4].rearrange("e (c p) d -> p e c d", p=P))\
                    .then_inc(ffn_w, 16)

            def step(j, jh, par):
                if live(j, 2, STEPS):
                    act.wait_ge(gap_ready, j - 1)
                    nc.scalar.activation(rt[:, 7], rt[:, 6], ACT.Exp).then_inc(ex_ready, 1)
                if live(j, 0, STEPS):
                    act.wait_ge(adj_in[par], 16 * (jh + 1))
                    if late(j, 1):
                        act.wait_ge(ta_done, 2 * j)
                    nc.scalar.activation(AF[:], ADJ[:, par], ACT.Copy).then_inc(adj_f32, 1)
                    for h in range(2):
                        act.wait_ge(ta_done, 2 * j + h + 1)
                        if late(j, 1):
                            act.wait_ge(s2_done, 2 * (j - 1) + h + 1)
                        nc.scalar.activation(XNT[:, h], bank[0][:], ACT.Copy).then_inc(xnt_ready, 1)
                        nc.scalar.activation(AGT[:, h], bank[1][:], ACT.Copy).then_inc(xnt_ready, 1)
                    for h in range(2):
                        act.wait_ge(s2_done, 2 * j + h + 1)
                        if late(j, 1):
                            act.wait_ge(msg_used, HG * (2 * (j - 1) + h + 1))
                        nc.scalar.activation(U[:, h].rearrange("p g d -> p (g d)"), bank[2][:], ACT.Copy)\
                            .then_inc(u_ready, 1)
                if live(j, 1, STEPS):
                    for h in range(2):
                        act.wait_ge(xt_done, 2 * (j - 1) + h + 1)
                        if late(j, 2):
                            act.wait_ge(lg_done, 2 * (j - 2) + h + 1)
                        nc.scalar.activation(XTT[:, h], bank[0][:], ACT.Copy).then_inc(xtt_ready, 1)

            stage_a(act, step)

            def tile(t, th, q):
                def high(t, q):
                    act.wait_ge(xtb_done, t + 1)
                    if late(t, 2):
                        act.wait_ge(z_done, 2 * (t - 1))
                    nc.scalar.activation(xh[:, q % 2], bank[6 + q % 2][:, 0:P], ACT.Copy).then_inc(xh_ready, 1)

                def gelu(t, q, k):
                    ex = act.value_load(tab[0:1, k, bass.ds(t, 1)], min_val=0, max_val=E - 1)
                    u = 2 * t + k
                    z = 2 * (q % 2) + k
                    act.wait_ge(z_done, u + 1)
                    if late(t, 2):
                        act.wait_ge(h_ready, 2 * (u - 3))
                    for c in range(C):
                        nc.scalar.activation(gl[:, z, c * P:(c + 1) * P], bank[z][:, c * P:(c + 1) * P], ACT.Gelu,
                                             bias=b1s[:, bass.ds(ex * C + c, 1)], scale=sc[:, 2:3])\
                            .then_inc(g_ready, 1)

                if isinstance(t, int) and t == 0:
                    act.wait_ge(weights_ready, 1)
                    act.wait_ge(tab_ready, 1)
                    high(t, q)
                if live(t, 0, TILES):
                    gelu(t, q, 0)
                if live(t, -1, TILES):
                    high(t + 1, (q + 1) % 4)
                if live(t, 0, TILES):
                    gelu(t, q, 1)

            stage_b(act, tile, TILES)

        @block.tensor
        def _(pe):
            mm = nc.tensor.matmul
            pe.wait_ge(consts, N_CONSTS)
            pe.wait_ge(ffn_w, 16 * N_FFN_W)
            ns = 2 * E + E * C
            nc.tensor.transpose(bank[7][:, 0:ns], small_rows[:, :], ident[0:ns, 0:ns]).then_inc(setup_pe, 1)
            pe.wait_ge(dve, 1)
            for e in range(E):
                for c in range(C):
                    mm(bank[6][:, e * C + c:e * C + c + 1], w1f[:, e, c * P:(c + 1) * P], small_cols[:, E + e:E + e + 1],
                       start=True, stop=True).then_inc(setup_pe, 1)
            pe.wait_ge(gnn_w, 16 * N_GNN_W)

            def step(j, jh, par):
                if live(j, 2, STEPS):
                    pe.wait_ge(oh_ready, j - 1)
                    if late(j, 3):
                        pe.wait_ge(pos_ready, j - 2)
                    mm(bank[7][:, 0:G * NP], tri[:], oh[:].rearrange("p g n -> p (g n)"), start=True, stop=False)
                    mm(bank[7][:, 0:G * NP], ones_b[:], pre[:, 0:G].rearrange("p g n -> p (g n)"), start=False,
                       stop=True).then_inc(rank_done, 1)
                if live(j, 0, STEPS):
                    for h in range(2):
                        pe.wait_ge(xn_ready, G * j + HG * (h + 1))
                        if h == 0:
                            pe.wait_ge(adj_f32, j + 1)
                            if late(j, 1):
                                pe.wait_ge(deg_used, j)
                            if late(j, 2):
                                pe.wait_ge(xtt_ready, 2 * (j - 1))
                        if h == 1 or late(j, 1):
                            pe.wait_ge(xnt_ready, 2 * (2 * j + h))
                        for g in range(HG):
                            gg = h * HG + g
                            nc.tensor.transpose(bank[0][:, g * P:(g + 1) * P], XN[:, gg, :], ident[:])
                            mm(bank[1][:, g * P:(g + 1) * P], XN[:, gg, :], AF[:, gg, :], start=True, stop=True)
                            last = mm(bank[5][:, gg:gg + 1], AF[:, gg, :], ones_f[:], start=True, stop=True)
                        last.then_inc(ta_done, 1)
                    for h in range(2):
                        pe.wait_ge(xnt_ready, 2 * (2 * j + h + 1))
                        if h == 1 or late(j, 1):
                            pe.wait_ge(u_ready, 2 * j + h)
                        if late(j, 1):
                            pe.wait_ge(msg_used, HG * (2 * (j - 1) + h + 1))
                        mm(bank[2][:], ones_row[:], bias_row[:].rearrange("o g d -> o (g d)"), start=True, stop=False)
                        for g in range(HG):
                            mm(bank[2][:, g * P:(g + 1) * P], XNT[:, h, g * P:(g + 1) * P], wupd[:], start=False,
                               stop=(g == HG - 1))
                        for g in range(HG):
                            last = mm(bank[3 + h][:, g * P:(g + 1) * P], AGT[:, h, g * P:(g + 1) * P], wmsg[:],
                                      start=True, stop=True)
                        last.then_inc(s2_done, 1)
                if live(j, 1, STEPS):
                    for h in range(2):
                        pe.wait_ge(xt_ready, (G + 1) * (j - 1) + HG * (h + 1))
                        if h == 0:
                            if live(j, 0, STEPS):
                                pe.wait_ge(xnt_ready, 2 * (2 * j + 2))
                            elif late(j, 2):
                                pe.wait_ge(xtt_ready, 2 * (j - 1))
                        else:
                            pe.wait_ge(xtt_ready, 2 * (j - 1) + 1)
                        for g in range(HG):
                            last = nc.tensor.transpose(bank[0][:, g * P:(g + 1) * P], XT[:, h * HG + g, :], ident[:])
                        last.then_inc(xt_done, 1)
                    for h in range(2):
                        pe.wait_ge(xtt_ready, 2 * (j - 1) + h + 1)
                        if late(j, 2):
                            pe.wait_ge(lg_used, j - 1)
                        for g in range(HG):
                            gg = h * HG + g
                            last = mm(bank[6][:, gg * E:(gg + 1) * E], XTT[:, h, g * P:(g + 1) * P], wr[:],
                                      start=True, stop=True)
                        last.then_inc(lg_done, 1)

            stage_a(pe, step)
            pe.wait_ge(pos_ready, STEPS)
            mm(bank[7][:, 0:NP], ones_b[:], pre[:, 0], start=True, stop=True).then_inc(total_done, 1)
            pe.wait_ge(fld_ready, 1)
            for f in range(3):
                mm(bank[5][0:1, f * P:(f + 1) * P], fld[:, f:f + 1], ident[:], start=True, stop=True)\
                    .then_inc(fld_row, 1)

            pe.wait_ge(weights_ready, 1)
            pe.wait_ge(tab_ready, 1)

            def turn(t, q):
                pe.wait_ge(xs_ready, t + 1)
                if late(t, 2):
                    pe.wait_ge(xl_ready, t - 1)
                nc.tensor.transpose(bank[6 + q % 2][:, 0:P], xs[:, q % 2, :], ident[:]).then_inc(xtb_done, 1)

            def up(t, q, k):
                ex = pe.value_load(tab[0:1, k, bass.ds(t, 1)], min_val=0, max_val=E - 1)
                u, z = 2 * t + k, 2 * (q % 2) + k
                if k == 0:
                    pe.wait_ge(xh_ready, t + 1)
                    pe.wait_ge(xl_ready, t + 1)
                if late(t, 2):
                    pe.wait_ge(g_ready, C * (u - 3))
                for c in range(C):
                    zz = bank[z][:, c * P:(c + 1) * P]
                    wh = w1h[:, bass.ds(ex, 1), c, :]
                    mm(zz, wh, xh[:, q % 2], start=True, stop=False)
                    mm(zz, wh, xl[:, q % 2], start=False, stop=False)
                    last = mm(zz, w1l[:, bass.ds(ex, 1), c, :], xh[:, q % 2], start=False, stop=True)
                last.then_inc(z_done, 1)

            def down(t, q, k):
                ex = pe.value_load(tab[0:1, k, bass.ds(t, 1)], min_val=0, max_val=E - 1)
                u, z = 2 * t + k, 2 * (q % 2) + k
                pe.wait_ge(h_ready, 2 * (u + 1))
                if k == 0 and late(t, 2):
                    pe.wait_ge(o_ready, t - 1)
                y = bank[4 + q % 2][:, k * D:(k + 1) * D]
                mm(y, ones2[:], b2t[:, bass.ds(ex, 1), :], start=True, stop=False)
                for c in range(C):
                    mm(y, hh[:, z, c * P:(c + 1) * P], w2h[:, bass.ds(ex, 1), c, :], start=False, stop=False)
                    mm(y, hh[:, z, c * P:(c + 1) * P], w2l[:, bass.ds(ex, 1), c, :], start=False, stop=False)
                    last = mm(y, hl[:, z, c * P:(c + 1) * P], w2h[:, bass.ds(ex, 1), c, :], start=False,
                              stop=(c == C - 1))
                last.then_inc(y_done, 1)

            def tile(t, th, q):
                if isinstance(t, int) and t == 0:
                    turn(t, q)
                if live(t, 0, TILES):
                    up(t, q, 0)
                if live(t, -1, TILES):
                    turn(t + 1, (q + 1) % 4)
                if live(t, 1, TILES):
                    down(t - 1, (q + 3) % 4, 0)
                if live(t, 0, TILES):
                    up(t, q, 1)
                if live(t, 1, TILES):
                    down(t - 1, (q + 3) % 4, 1)

            stage_b(pe, tile, TILES + 1)

        @block.vector
        def _(v):
            ts, tt, stt = nc.vector.tensor_scalar, nc.vector.tensor_tensor, nc.vector.scalar_tensor_tensor
            done = Done(v, dve)

            v.wait_ge(consts, N_CONSTS)
            v.wait_ge(setup_pe, 1)
            cols = done(nc.vector.tensor_copy(small_cols[:], bank[7][:, 0:2 * E + E * C]))
            v.wait_ge(ffn_w, 16 * N_FFN_W)
            v.wait_ge(gnn_w, 16 * N_GNN_W)
            m = done(nc.vector.tensor_reduce(amw[:], w1f[:], AX.X, ALU.max, apply_absolute_value=True))
            done(nc.vector.tensor_reduce(amax[:, 1:2], w2f[:].rearrange("p e c d -> p (e c d)"), AX.X, ALU.max,
                                         apply_absolute_value=True))
            done(nc.vector.tensor_reduce(amax[0:2, 3:4], b2row[:].rearrange("p e d -> p (e d)"), AX.X, ALU.max,
                                         apply_absolute_value=True))
            v.wait_ge(setup_pe, 1 + E * C)
            m = done(tt(b1s[:], bank[6][:, 0:E * C], small_cols[:, 2 * E:], ALU.add))
            done.wait(m)
            done(nc.vector.tensor_reduce(amax[:, 2:3], b1s[:], AX.X, ALU.max, apply_absolute_value=True))
            m = done(tt(amw[:], amw[:], small_cols[:, 0:E], ALU.mult))
            done.wait(m)
            nc.vector.tensor_reduce(amax[:, 0:1], amw[:], AX.X, ALU.max, apply_absolute_value=True)\
                .then_inc(amax_in, 1)
            v.wait_ge(amax_out, 1)
            m = done(ts(sc[:, 0:1], amax_all[:, 0:1], 1e-30, None, ALU.max))
            m = done(tt(sc[:, 1:2], amax_all[:, 1:2], amax_all[:, 3:4], ALU.max))
            done.wait(m)
            done(ts(sc[:, 1:2], sc[:, 1:2], 1e-30, None, ALU.max))
            m = done(stt(sc[:, 7:8], sc[:, 0:1], float(D), amax_all[:, 2:3], ALU.mult, ALU.add))
            done.wait(m)
            m = done(ts(sc[:, 8:9], sc[:, 7:8], 1.0, None, ALU.max))
            done.wait(m)
            done(ts(sc[:, 9:10].bitcast(I32), sc[:, 0:1].bitcast(I32), 0x7F800000, None, ALU.bitwise_and))
            done(ts(sc[:, 10:11].bitcast(I32), sc[:, 1:2].bitcast(I32), 0x7F800000, None, ALU.bitwise_and))
            m = done(ts(sc[:, 11:12].bitcast(I32), sc[:, 8:9].bitcast(I32), 0x7F800000, None, ALU.bitwise_and))
            done.wait(m)
            m = done(nc.vector.reciprocal(sc[:, 12:15], sc[:, 9:12]))
            done.wait(m)
            done(ts(sc[:, 2:3], sc[:, 9:10], 2.0 ** -9, None, ALU.mult))
            done(ts(sc[:, 3:4], sc[:, 12:13], 2.0 ** 9, None, ALU.mult))
            done(ts(sc[:, 4:5], sc[:, 13:14], 2.0 ** 9, None, ALU.mult))
            done(ts(sc[:, 5:6], sc[:, 14:15], 2.0 ** 14, None, ALU.mult))
            m = done(tt(sc[:, 6:7], sc[:, 10:11], sc[:, 11:12], ALU.mult))
            done.wait(m)
            done(ts(sc[:, 6:7], sc[:, 6:7], 2.0 ** -23, None, ALU.mult))
            done(ts(gsc[:], small_cols[:, 0:E], sc[:, 3:4], None, ALU.mult))
            done(ts(b2sc[:], b2row[:], sc[0:2, 4:5], None, ALU.mult))
            m = done(ts(ones2[0:2, :], ident[0:2, :], 0.0, sc[0:2, 5:6], ALU.mult, ALU.add))
            done.wait(m)
            for e in range(E):
                w = w1h[:, e].rearrange("p c h -> p (c h)")
                done(ts(w, w1f[:, e], gsc[:, e:e + 1], None, ALU.mult))
            done(ts(w2h[:].rearrange("p e c d -> p (e c d)"), w2f[:].rearrange("p e c d -> p (e c d)"),
                    sc[:, 4:5], None, ALU.mult))
            m = done(nc.vector.tensor_copy(b2hi[:], b2sc[:]))
            done.wait(m)
            for e in range(E):
                done(stt(w1l[:, e].rearrange("p c h -> p (c h)"), w1f[:, e], gsc[:, e:e + 1],
                         w1h[:, e].rearrange("p c h -> p (c h)"), ALU.mult, ALU.subtract))
            done(stt(w2l[:].rearrange("p e c d -> p (e c d)"), w2f[:].rearrange("p e c d -> p (e c d)"),
                     sc[:, 4:5], w2h[:].rearrange("p e c d -> p (e c d)"), ALU.mult, ALU.subtract))
            m = done(tt(b2hi32[:], b2sc[:], b2hi[:], ALU.subtract))
            done.wait(m)
            m = done(tt(b2hi32[:], b2hi32[:], b2hi[:], ALU.subtract))
            done.wait(m)
            stt(b2t[0:2].rearrange("p e d -> p (e d)"), b2hi32[:].rearrange("p e d -> p (e d)"), halfsel[:, 0:1],
                b2hi[:].rearrange("p e d -> p (e d)"), ALU.mult, ALU.add).then_inc(weights_ready, 1)

            a0 = [done.n, 0]

            def rebase(i):
                if a0[1] == 0:
                    a0[1] = done.n - a0[0]
                base = a0[0] + a0[1]
                done.rebase(base + (i - 1) * DVE_TURN)

            l, q1, o1_, q2 = (L[:, i] for i in range(4))
            m1, k1, m2, k2, hi, key, gap, ex, den, w1_, w2_, sw, dw, sdw, lo = (rt[:, i] for i in range(15))
            shape = [P, G, E]

            def wide(a):
                return a.unsqueeze(2).to_broadcast(shape)

            def step(j, jh, par):
                if live(j, 2, STEPS):
                    v.wait_ge(lg_done, 2 * (j - 1))
                    tt(l, bank[6][:, 0:G * E].rearrange("p (g e) -> p g e", g=G),
                       brb[:].unsqueeze(1).to_broadcast(shape), ALU.add).then_inc(lg_used, 1)
                    v.wait_ge(lg_used, j - 1)
                    m = done(nc.vector.tensor_reduce(m1, l, AX.X, ALU.max))
                    done.wait(m)
                    m = done(tt(q1, l, wide(m1), ALU.is_equal))
                    done.wait(m)
                    m = done(tt(q1, q1, rev[:], ALU.mult))
                    done.wait(m)
                    m = done(nc.vector.tensor_reduce(k1, q1, AX.X, ALU.max))
                    done.wait(m)
                    m = done(tt(o1_, rev[:], wide(k1), ALU.is_equal))
                    done.wait(m)
                    m = done(stt(q2, o1_, BIG, l, ALU.mult, ALU.add))
                    done.wait(m)
                    m = done(nc.vector.tensor_reduce(m2, q2, AX.X, ALU.max))
                    done.wait(m)
                    tt(gap, m2, m1, ALU.subtract).then_inc(gap_ready, 1)
                    m = done(tt(q1, q2, wide(m2), ALU.is_equal))
                    done.wait(m)
                    m = done(tt(q1, q1, rev[:], ALU.mult))
                    done.wait(m)
                    m = done(nc.vector.tensor_reduce(k2, q1, AX.X, ALU.max))
                    done.wait(m)
                    done(tt(sw, k2, k1, ALU.is_gt))
                    done(tt(lo, k1, k2, ALU.min))
                    m = done(tt(hi, k1, k2, ALU.max))
                    done.wait(m)
                    m = done(stt(key, hi, float(E), lo, ALU.mult, ALU.add))
                    done.wait(m)
                    m = done(tt(oh[:], keys[:], key.unsqueeze(2).to_broadcast([P, G, NP]), ALU.is_equal))
                    done.wait(m)
                    for g in range(G):
                        i_ = tt(pre[:, g + 1], pre[:, g], oh[:, g], ALU.add)
                        if g < G - 1:
                            m = done(i_)
                            done.wait(m)
                        else:
                            i_.then_inc(oh_ready, 1)
                if live(j, 0, STEPS):
                    v.wait_ge(x_in[par], 16 * (jh + 1))
                    for g in range(G):
                        m = done(nc.vector.bn_stats(st1[:, g], X[:, par, g]))
                    wait_alone(v, dve, m)
                    for g in range(G):
                        m = done(nc.vector.bn_aggr(mv1[:, g], st1[:, g]))
                    done.wait(m)
                    if late(j, 1):
                        v.wait_ge(r1_ready, j)
                    ts(ve1[:], mv1[:, :, 1], EPS, None, ALU.add).then_inc(ve1_ready, 1)
                if live(j, 1, STEPS):
                    p1 = 1 - par
                    v.wait_ge(ta_done, 2 * j)
                    m = done(ts(dg[:, 0], bank[5][:, 0:G], 1.0, None, ALU.max))
                    done.wait(m)
                    m = done(nc.vector.reciprocal(dg[:, 1], dg[:, 0]))
                    done.wait(m)
                    stt(dg[:, 2], bank[5][:, 0:G], 0.0, dg[:, 1], ALU.is_gt, ALU.mult).then_inc(deg_used, 1)
                    v.wait_ge(deg_used, j)
                    for h in range(2):
                        v.wait_ge(s2_done, 2 * (j - 1) + h + 1)
                        v.wait_ge(u_ready, 2 * (j - 1) + h + 1)
                        for g in range(HG):
                            gg = h * HG + g
                            stt(T[:, h, g], bank[3 + h][:, g * P:(g + 1) * P], dg[:, 2, gg:gg + 1], U[:, h, g],
                                ALU.mult, ALU.add).then_inc(msg_used, 1)
                    for h in range(2):
                        v.wait_ge(msg_used, HG * (2 * (j - 1) + h + 1))
                        if late(j, 2):
                            v.wait_ge(rows_free, j - 1)
                        stt(SR[:, p1, h * HG:(h + 1) * HG, 0:D], T[:, h], 0.0, X[:, p1, h * HG:(h + 1) * HG],
                            ALU.max, ALU.add).then_inc(x2_ready, 1)
                    v.wait_ge(x2_ready, 2 * j)
                    for g in range(G):
                        m = done(nc.vector.bn_stats(st2[:, g], SR[:, p1, g, 0:D]))
                    wait_alone(v, dve, m)
                    for g in range(G):
                        m = done(nc.vector.bn_aggr(mv2[:, g], st2[:, g]))
                    done.wait(m)
                    if late(j, 2):
                        v.wait_ge(r2_ready, j - 1)
                    m = done(ts(ve2[:, 0], mv2[:, :, 1], EPS, None, ALU.add))
                    done.wait(m)
                    stt(ve2[:, 1], ve2[:, 0], EPS, mv2[:, :, 1], ALU.mult, ALU.add).then_inc(ve2_ready, 1)
                    done(nc.vector.tensor_copy(SR[:, p1, :, MU], mv2[:, :, 0]))
                if live(j, 0, STEPS):
                    v.wait_ge(r1_ready, j + 1)
                    if late(j, 1):
                        v.wait_ge(ta_done, 2 * j)
                    for g in range(G):
                        ts(XN[:, g], X[:, par, g], mv1[:, g, 0:1], r1[:, g:g + 1], ALU.subtract, ALU.mult)\
                            .then_inc(xn_ready, 1)
                if live(j, 1, STEPS):
                    p1 = 1 - par
                    v.wait_ge(r2_ready, j)
                    if late(j, 2):
                        v.wait_ge(xt_done, 2 * (j - 1))
                    for g in range(G):
                        ts(XT[:, g], SR[:, p1, g, 0:D], mv2[:, g, 0:1], r2[:, 0, g:g + 1], ALU.subtract, ALU.mult)\
                            .then_inc(xt_ready, 1)
                    nc.vector.tensor_copy(SR[:, p1, :, RS], r2[:, 1]).then_inc(xt_ready, 1)
                if live(j, 2, STEPS):
                    v.wait_ge(ex_ready, j - 1)
                    m = done(ts(den, ex, 1.0, None, ALU.add))
                    done.wait(m)
                    m = done(nc.vector.reciprocal(w1_, den))
                    done.wait(m)
                    m = done(ts(w1_, w1_, sc[:, 6:7], None, ALU.mult))
                    done.wait(m)
                    m = done(tt(w2_, ex, w1_, ALU.mult))
                    done.wait(m)
                    m = done(tt(dw, w2_, w1_, ALU.subtract))
                    done.wait(m)
                    m = done(tt(sdw, sw, dw, ALU.mult))
                    done.wait(m)
                    done(tt(SR[:, par, :, WA], w1_, sdw, ALU.add))
                    done(tt(SR[:, par, :, WB], w2_, sdw, ALU.subtract))
                    done(nc.vector.tensor_copy(SR[:, par, :, TOK].bitcast(I32), tok[:]))
                    v.wait_ge(rank_done, j - 1)
                    m = done(nc.vector.tensor_copy(pre[:, 0], pre[:, G]))
                    m = done(tt(rk[:], bank[7][:, 0:G * NP].rearrange("p (g n) -> p g n", g=G), rowb[:], ALU.add))
                    done.wait(m)
                    m = done(tt(rk[:], rk[:], oh[:], ALU.mult))
                    m = done(ts(tok[:], tok[:], float(G * N), None, ALU.add))
                    done.wait(m)
                    with nc.allow_low_precision(reason="sums of whole numbers below 2**24"):
                        nc.vector.tensor_reduce(pos[:, par], rk[:], AX.X, ALU.add).then_inc(pos_ready, 1)
                if not isinstance(j, int) and par == 1:
                    assert done.n == DVE_TURN, done.n

            stage_a(v, step, rebase)

            v.wait_ge(pos_ready, STEPS)
            done(nc.vector.memset(fld[:, 3:4], 0.0))
            v.wait_ge(total_done, 1)
            done(nc.vector.tensor_copy(cntf[:], bank[7][:, 0:NP]))
            m = done(ts(cnti[:], bank[7][:, 0:NP], float(P - 1), None, ALU.add))
            done.wait(m)
            tt(fill[:], cntf[0:1], rowb[0:1, 0], ALU.add).then_inc(fill_ready, 1)
            m = done(ts(cnti[:], cnti[:], 7, None, ALU.logical_shift_right))
            done.wait(m)
            m = done(nc.vector.tensor_copy(ntf[:], cnti[:]))
            done.wait(m)
            m = done(nc.vector.tensor_copy(inc[:, 0], ntf[:]))
            done.wait(m)
            a, s = 0, 1
            while s < NP:
                done(tt(inc[:, 1 - a, s:], inc[:, a, s:], inc[:, a, :NP - s], ALU.add))
                m = done(nc.vector.tensor_copy(inc[:, 1 - a, :s], inc[:, a, :s]))
                done.wait(m)
                a, s = 1 - a, 2 * s
            last = inc[:, a]
            m = done(tt(tw[:, 0], last, ntf[:], ALU.subtract))
            done.wait(m)
            done(ts(tw[:, 1], tw[:, 0], tcol[:, 0:1], None, ALU.is_le))
            m = done(ts(tw[:, 2], last, tcol[:, 0:1], None, ALU.is_gt))
            done.wait(m)
            m = done(tt(tw[:, 1], tw[:, 1], tw[:, 2], ALU.mult))
            m = done(ts(tw[:, 3], tw[:, 0], tcol[:, 0:1], -float(P), ALU.subtract, ALU.mult))
            done.wait(m)
            m = done(tt(tw[:, 3], tw[:, 3], rowb[:, 0], ALU.add))
            done.wait(m)
            m = done(ts(tw[:, 3], tw[:, 3], float(PAD_SEG), None, ALU.subtract))
            done.wait(m)
            m = done(tt(tw[:, 3], tw[:, 3], tw[:, 1], ALU.mult))
            done(tt(tw[:, 0], exp_a[:], tw[:, 1], ALU.mult))
            m = done(tt(tw[:, 2], exp_b[:], tw[:, 1], ALU.mult))
            done.wait(m)
            done(nc.vector.tensor_reduce(fld[:, 0:1], tw[:, 0], AX.X, ALU.add))
            done(nc.vector.tensor_reduce(fld[:, 1:2], tw[:, 2], AX.X, ALU.add))
            m = done(nc.vector.tensor_reduce(fld[:, 2:3], tw[:, 3], AX.X, ALU.add))
            done.wait(m)
            ts(fld[:, 2:3], fld[:, 2:3], float(PAD_SEG), None, ALU.add).then_inc(fld_ready, 1)
            v.wait_ge(fld_row, 3)
            nc.vector.tensor_copy(tab[:].rearrange("o f t -> o (f t)"), bank[5][0:1, 0:3 * P]).then_inc(tab_ready, 1)

            def normal(t, th, q):
                v.wait_ge(ra_in[q], 16 * (th + 1))
                if late(t, 2):
                    v.wait_ge(xtb_done, t - 1)
                ts(xs[:, q % 2], RA[:, q, 0:D], RA[:, q, MU:MU + 1], RA[:, q, RS:RS + 1], ALU.subtract, ALU.mult)\
                    .then_inc(xs_ready, 1)

            def low(t, q):
                v.wait_ge(xh_ready, t + 1)
                if late(t, 2):
                    v.wait_ge(z_done, 2 * (t - 1))
                tt(xl[:, q % 2], bank[6 + q % 2][:, 0:P], xh[:, q % 2], ALU.subtract).then_inc(xl_ready, 1)

            def halves(t, q, k):
                u, z = 2 * t + k, 2 * (q % 2) + k
                v.wait_ge(g_ready, C * (u + 1))
                if late(t, 2):
                    v.wait_ge(y_done, u - 3)
                ts(hh[:, z], gl[:, z], sc[:, 5:6], None, ALU.mult).then_inc(h_ready, 1)
                v.wait_ge(h_ready, 2 * u + 1)
                stt(hl[:, z], gl[:, z], sc[:, 5:6], hh[:, z], ALU.mult, ALU.subtract).then_inc(h_ready, 1)

            def combine(t, th, q):
                v.wait_ge(y_done, 2 * (t + 1))
                v.wait_ge(rc_in[q], 16 * (th + 1))
                if late(t, 4):
                    v.wait_ge(stored[q], 16 * th)
                y = bank[4 + q % 2]
                m = done(stt(o1[:, q % 2], y[:, 0:D], RC[:, q, WA:WA + 1], RC[:, q, 0:D], ALU.mult, ALU.add))
                done.wait(m)
                stt(o[:, q], y[:, D:2 * D], RC[:, q, WB:WB + 1], o1[:, q % 2], ALU.mult, ALU.add)\
                    .then_inc(o_ready, 1)

            def tile(t, th, q):
                if isinstance(t, int) and t == 0:
                    normal(0, 0, 0)
                    normal(1, 0, 1)
                    low(0, 0)
                if live(t, 0, TILES):
                    halves(t, q, 0)
                if live(t, -1, TILES):
                    low(t + 1, (q + 1) % 4)
                if live(t, -2, TILES):
                    normal(t + 2, th + (1 if q >= 2 else 0), (q + 2) % 4)
                if live(t, 2, TILES):
                    combine(t - 2, th - (1 if q < 2 else 0), (q + 2) % 4)
                if live(t, 0, TILES):
                    halves(t, q, 1)

            b0 = [done.base + done.n, 0]

            def rebase_b(i):
                done.rebase(b0[0] + (B_FIRST - 2) + (i - 1) * 4)

            stage_b(v, tile, TILES + 2, rebase_b)


N_CONSTS = 12 + 3 + 3 * (E - 1) + 5
DVE_TURN = 142
RMAX = bass.bass_isa.ReduceOp.max

_INS = ["x", "adj", "L0_gnn_W_msg", "L0_gnn_W_upd", "L0_gnn_bias", "L0_ffn_Wr", "L0_ffn_br", "L0_ffn_ln_g",
        "L0_ffn_ln_b", "L0_ffn_W1", "L0_ffn_b1", "L0_ffn_W2", "L0_ffn_b2"]


def kernel(**inputs):
    import numpy as _np
    import concourse.bacc as _bacc
    from concourse.bass_utils import run_bass_kernel_spmd as _run

    nc = _bacc.Bacc("TRN2", target_bir_lowering=False, num_devices=1)
    arrays, args = {}, []
    for name in _INS:
        a = _np.ascontiguousarray(inputs[name])
        arrays[f"in_{name}"] = a
        args.append(nc.dram_tensor(f"in_{name}", a.shape, mybir.dt.from_np(a.dtype), kind="ExternalInput").ap())
    out = nc.dram_tensor("out_rows", (TOKENS, D), F32, kind="ExternalOutput").ap()
    moe_gnn(nc, *args, out)
    r = _run(nc, [arrays], core_ids=[0])
    return r.results[0]["out_rows"].reshape(B, N, D)
```

```python
import numpy as np
import concourse.bass as bass
from concourse import mybir
from contextlib import ExitStack

F32, F16, BF16, I32 = mybir.dt.float32, mybir.dt.float16, mybir.dt.bfloat16, mybir.dt.int32
ALU = mybir.AluOpType
ACT = mybir.ActivationFunctionType
AX = mybir.AxisListType

P = 128
B, N, D = 64, 128, 128
E, H = 8, 512
C = H // P
TOKENS = B * N
EPS = 1e-5

G = 8
HG = G // 2
STEPS = B // G

PAIRS = [(a, b) for a in range(E) for b in range(a + 1, E)]
NP = len(PAIRS)
SEG = TOKENS + P
PAD_SEG = NP * SEG
TILES = TOKENS // P + NP - 1

MU, RS, WA, WB, TOK, ROW = D, D + 1, D + 2, D + 3, D + 4, D + 8

BIG = -3.0e38


class Done:

    def __init__(self, engine, sem):
        self.engine, self.sem, self.base, self.n = engine, sem, 0, 0

    def __call__(self, instruction):
        instruction.then_inc(self.sem, 1)
        self.n += 1
        return self.base + self.n

    def wait(self, mark):
        self.engine.wait_ge(self.sem, mark)

    def rebase(self, base):
        self.base, self.n = base, 0


def moe_gnn(nc, x, adj, W_msg, W_upd, bias, Wr, br, ln_g, ln_b, W1, b1, W2, b2, out):
    ctx = ExitStack()
    with ctx:
        def sb(name, shape, dt):
            return ctx.enter_context(nc.sbuf_tensor(name, shape, dt))

        def sem(name):
            return ctx.enter_context(nc.semaphore(name))

        rows = nc.dram_tensor("rows", (PAD_SEG + P, ROW), F32, kind="Internal").ap()

        ident = sb("ident", [P, P], F32)
        ones_f = sb("ones_f", [P, 1], F32)
        ones_row = sb("ones_row", [1, P], F32)
        tri = sb("tri", [P, P], BF16)
        ones_b = sb("ones_b", [P, P], BF16)
        rev = sb("rev", [P, G, E], F32)
        keys = sb("keys", [P, G, NP], F32)
        rowb = sb("rowb", [P, G, NP], F32)
        exp_a = sb("exp_a", [P, NP], F32)
        exp_b = sb("exp_b", [P, NP], F32)
        tcol = sb("tcol", [P, 1], F32)
        tok = sb("tok", [P, G], F32)
        nhalf = sb("nhalf", [P, 2 * G], F32)
        padrow = sb("padrow", [P, ROW], F32)

        wmsg = sb("wmsg", [P, D], F32)
        wupd = sb("wupd", [P, D], F32)
        wr = sb("wr", [P, E], F32)
        brb = sb("brb", [P, E], F32)
        bias_row = sb("bias_row", [1, HG, D], F32)
        w1f = sb("w1f", [P, E, H], F32)
        w2f = sb("w2f", [P, E, C, D], F32)
        w1h = [sb(f"w1h{c}", [P, E, P], F16) for c in range(C)]
        w1l = [sb(f"w1l{c}", [P, E, P], F16) for c in range(C)]
        w2h = [sb(f"w2h{c}", [P, E, D], F16) for c in range(C)]
        w2l = [sb(f"w2l{c}", [P, E, D], F16) for c in range(C)]
        b1c = [sb(f"b1c{c}", [P, E], F32) for c in range(C)]
        small_rows = sb("small_rows", [2 * E + E * C, P], F32)
        small_cols = sb("small_cols", [P, 2 * E + E * C], F32)
        b2row = sb("b2row", [2, E, D], F32)
        b2sc = sb("b2sc", [2, E, D], F32)
        b2hi = sb("b2hi", [2, E, D], F16)
        b2t = sb("b2t", [P, E, D], F16)
        b2hi32 = sb("b2hi32", [2, E, D], F32)
        halfsel = sb("halfsel", [2, 1], F32)
        ones2 = sb("ones2", [P, P], F16)
        b1s = sb("b1s", [P, C, E], F32)
        gsc = sb("gsc", [P, E], F32)
        amax = sb("amax", [P, 4], F32)
        amax_all = sb("amax_all", [P, 4], F32)
        amw = sb("amw", [P, E], F32)
        sc = sb("sc", [P, 16], F32)

        X = sb("X", [P, 2, G, D], F32)
        ADJ = sb("ADJ", [P, 2, G, N], I32)
        AF = sb("AF", [P, G, N], F32)
        XN = sb("XN", [P, G, D], F32)
        XNT = sb("XNT", [P, 2, HG * P], F32)
        AGT = sb("AGT", [P, 2, HG * P], F32)
        U = sb("U", [P, 2, HG, D], F32)
        T = sb("T", [P, 2, HG, D], F32)
        SR = sb("SR", [P, 2, G, ROW], F32)
        XT = sb("XT", [P, G, D], F32)
        XTT = sb("XTT", [P, 2, HG * P], F32)
        st1 = sb("st1", [P, G, 6], F32)
        mv1 = sb("mv1", [P, G, 2], F32)
        ve1 = sb("ve1", [P, G], F32)
        r1 = sb("r1", [P, G], F32)
        st2 = sb("st2", [P, G, 6], F32)
        mv2 = sb("mv2", [P, G, 2], F32)
        ve2 = sb("ve2", [P, 2, G], F32)
        r2 = sb("r2", [P, 2, G], F32)
        dg = sb("dg", [P, 3, G], F32)
        L = sb("L", [P, 4, G, E], F32)
        rt = sb("rt", [P, 20, G], F32)
        oh = sb("oh", [P, G, NP], BF16)
        pre = sb("pre", [P, G + 1, NP], BF16)
        rk = sb("rk", [P, G, NP], F32)
        pos = sb("pos", [P, 2, G], I32)

        cntf = sb("cntf", [P, NP], F32)
        cnti = sb("cnti", [P, NP], I32)
        ntf = sb("ntf", [P, NP], F32)
        inc = sb("inc", [P, 2, NP], F32)
        tw = sb("tw", [P, 4, NP], F32)
        fld = sb("fld", [P, 4], F32)
        experts = sb("experts", [1, P, 4], I32)
        tile_row = sb("tile_row", [1, P], I32)
        fill = sb("fill", [1, NP], I32)

        RA = sb("RA", [P, 4, ROW], F32)
        RC = sb("RC", [P, 4, ROW], F32)
        xs = sb("xs", [P, 2, D], F32)
        xh = sb("xh", [P, 4, P], F16)
        xl = sb("xl", [P, 4, P], F16)
        gl = sb("gl", [P, 4, H], F32)
        hh = sb("hh", [P, 4, H], F16)
        hl = sb("hl", [P, 4, H], F16)
        o = sb("o", [P, 4, D], F32)
        o1 = sb("o1", [P, 2, D], F32)

        bank = [ctx.enter_context(nc.psum_tensor(f"bank{i}", [P, 512], F32)) for i in range(8)]

        consts = sem("consts")
        gnn_w = sem("gnn_w")
        ffn_w = sem("ffn_w")
        x_in = [sem(f"x_in{i}") for i in range(2)]
        adj_in = [sem(f"adj_in{i}") for i in range(2)]
        dve = sem("dve_done")
        setup_pe = sem("setup_pe")
        amax_in = sem("amax_in")
        amax_out = sem("amax_out")
        ve1_ready, r1_ready = sem("ve1_ready"), sem("r1_ready")
        ve2_ready, r2_ready = sem("ve2_ready"), sem("r2_ready")
        xn_ready, xt_ready = sem("xn_ready"), sem("xt_ready")
        ta_done, s2_done, xt_done, lg_done = sem("ta_done"), sem("s2_done"), sem("xtr_done"), sem("lg_done")
        adj_f32 = sem("adj_f32")
        xnt_ready, u_ready, xtt_ready = sem("xnt_ready"), sem("u_ready"), sem("xtt_ready")
        deg_used, msg_used, x2_ready = sem("deg_used"), sem("msg_used"), sem("x2_ready")
        lg_used, gap_ready, ex_ready = sem("lg_used"), sem("gap_ready"), sem("ex_ready")
        oh_ready, rank_done, pos_ready = sem("oh_ready"), sem("rank_done"), sem("pos_ready")
        rows_free = sem("rows_free")
        scattered = [sem(f"scattered{i}") for i in range(2)]
        total_done, fld_ready, fld_row = sem("total_done"), sem("fld_ready"), sem("fld_row")
        tab_ready, fill_ready, padded = sem("tab_ready"), sem("fill_ready"), sem("padded")
        weights_ready = sem("weights_ready")
        ra_in = [sem(f"ra_in{i}") for i in range(4)]
        rc_in = [sem(f"rc_in{i}") for i in range(4)]
        xs_ready, xtb_done, xh_ready, xl_ready = sem("xs_ready"), sem("xtb_done"), sem("xh_ready"), sem("xl_ready")
        z_done, g_ready, h_ready, y_done = sem("z_done"), sem("g_ready"), sem("h_ready"), sem("y_done")
        o_ready = sem("o_ready")
        passed = sem("passed")
        stored = [sem(f"stored{i}") for i in range(4)]

        block = ctx.enter_context(nc.Block())

        N_GNN_W = 5 + HG
        N_FFN_W = 6

        def wait_alone(eng, semaphore, value):
            eng.wait_ge(semaphore, value)
            eng.sem_inc(passed, 1)

        def live(j, lag, n):
            return not isinstance(j, int) or 0 <= j - lag < n

        def late(j, k):
            return not isinstance(j, int) or j - k >= 0

        def stage_a(step):
            for j in range(STEPS + 2):
                step(j, j // 2, j % 2)

        B_FIRST = 8
        B_TURNS = (TILES - 3 - B_FIRST) // 4
        B_LAST = B_FIRST + 4 * B_TURNS

        def near(t, th, q, k):
            return t + k, th + (q + k) // 4, (q + k) % 4

        def stage_b(eng, step, last, rebase=None):
            for t in range(B_FIRST):
                step(t, t // 4, t % 4)
            with eng.Fori(B_FIRST // 4, B_LAST // 4) as i:
                if rebase:
                    rebase(i)
                for k in range(4):
                    step(4 * i + k, i, k)
            if rebase:
                rebase(B_LAST // 4)
            for t in range(B_LAST, last):
                step(t, t // 4, t % 4)

        def load_experts(eng, t, n):
            return nc.values_load_multi_w_load_instructions(
                experts[0:1, bass.ds(t, 1), 0:n].rearrange("o t f -> o (t f)"), engines=[eng.engine], min_val=0,
                max_val=E - 1, skip_runtime_bounds_check_because="an expert's index times 0 or 1")[1]

        @block.sync
        def _(sp):
            def load(j, jh, par):
                if not live(j, 0, STEPS):
                    return
                if late(j, 2):
                    wait_alone(sp, x2_ready, 2 * (j - 1))
                    wait_alone(sp, adj_f32, j - 1)
                sp.dma_start(X[:, par], x[bass.ds(j * G, G)].rearrange("g n f -> n g f"))\
                    .then_inc(x_in[par], 16)
                sp.dma_start(ADJ[:, par], adj[bass.ds(j * G, G)].rearrange("g n f -> n g f"))\
                    .then_inc(adj_in[par], 16)

            for j in range(STEPS):
                load(j, j // 2, j % 2)

            sp.wait_ge(consts, N_CONSTS)
            sp.dma_start(rows[PAD_SEG:PAD_SEG + P, :], padrow[:, :]).then_inc(padded, 16)
            sp.wait_ge(fill_ready, 1)
            with sp.Fori(0, NP) as i:
                at = sp.value_load(fill[0:1, bass.ds(i, 1)], min_val=0, max_val=PAD_SEG - P)
                sp.dma_start(rows[bass.ds(at, P), :], padrow[:, :]).then_inc(padded, 16)
            for par in range(2):
                sp.wait_ge(scattered[par], 16 * G * STEPS // 2)
            sp.wait_ge(padded, 16 * (NP + 1))
            sp.wait_ge(tab_ready, 7)

            def load_rows(t, th, q):
                if live(t, 0, TILES):
                    at = sp.value_load(tile_row[0:1, bass.ds(t, 1)], min_val=0, max_val=PAD_SEG)
                    if late(t, 4):
                        wait_alone(sp, o_ready, t - 3)
                        wait_alone(sp, stored[q], 16 * th)
                    sp.dma_start(RC[:, q], rows[bass.ds(at, P), :]).then_inc(rc_in[q], 16)
                t3, _, q3 = near(t, th, q, 3)
                if live(t, -3, TILES):
                    load_ra(t3, q3)

            def load_ra(t, q):
                at = sp.value_load(tile_row[0:1, bass.ds(t, 1)], min_val=0, max_val=PAD_SEG)
                if late(t, 4):
                    wait_alone(sp, xs_ready, t - 3)
                sp.dma_start(RA[:, q], rows[bass.ds(at, P), :]).then_inc(ra_in[q], 16)

            for t in range(3):
                load_ra(t, t)
            stage_b(sp, load_rows, TILES)
            for q in range(4):
                sp.wait_ge(stored[q], 16 * len(range(q, TILES, 4)))

        @block.gpsimd
        def _(pool):
            n = [0]

            def const(instruction):
                instruction.then_inc(consts, 1)
                n[0] += 1

            def settle():
                pool.wait_ge(consts, n[0])

            const(pool.memset(ident[:], 0.0))
            const(pool.memset(ones_f[:], 1.0))
            const(pool.memset(ones_row[:], 1.0))
            const(pool.memset(tri[:], 1.0))
            const(pool.memset(ones_b[:], 1.0))
            const(pool.memset(nhalf[:], -0.5))
            const(pool.memset(padrow[:], 0.0))
            const(pool.memset(pre[:], 0.0))
            const(pool.memset(SR[:], 0.0))
            const(pool.memset(b2t[:], 0.0))
            const(pool.memset(ones2[:], 0.0))
            const(pool.memset(amax[:], 0.0))
            settle()
            const(pool.affine_select(out=ident[:], in_=ident[:], compare_op=ALU.not_equal, fill=1.0, base=0,
                                     pattern=[[-1, P]], channel_multiplier=1))
            const(pool.affine_select(out=tri[:], in_=tri[:], compare_op=ALU.is_ge, fill=0.0, base=-1,
                                     pattern=[[1, P]], channel_multiplier=-1))
            const(pool.iota(rev[:], pattern=[[0, G], [-1, E]], base=E, channel_multiplier=0,
                            allow_small_or_imprecise_dtypes=True))
            off = 0
            for a in range(E - 1):
                k = E - 1 - a
                const(pool.iota(keys[:, :, off:off + k], pattern=[[0, G], [-1, k]],
                                base=E * (E - a) + E - (a + 1), channel_multiplier=0,
                                allow_small_or_imprecise_dtypes=True))
                const(pool.iota(exp_a[:, off:off + k], pattern=[[0, k]], base=a, channel_multiplier=0,
                                allow_small_or_imprecise_dtypes=True))
                const(pool.iota(exp_b[:, off:off + k], pattern=[[1, k]], base=a + 1, channel_multiplier=0,
                                allow_small_or_imprecise_dtypes=True))
                off += k
            const(pool.iota(rowb[:], pattern=[[0, G], [SEG, NP]], base=0, channel_multiplier=0,
                            allow_small_or_imprecise_dtypes=True))
            const(pool.iota(tcol[:], pattern=[[0, 1]], base=0, channel_multiplier=1,
                            allow_small_or_imprecise_dtypes=True))
            const(pool.iota(halfsel[:], pattern=[[0, 1]], base=0, channel_multiplier=1,
                            allow_small_or_imprecise_dtypes=True))
            const(pool.iota(tok[:], pattern=[[P, G]], base=0, channel_multiplier=1,
                            allow_small_or_imprecise_dtypes=True))
            const(pool.iota(padrow[:, TOK:TOK + 1].bitcast(I32), pattern=[[0, 1]], base=TOKENS,
                            channel_multiplier=0))
            assert n[0] == N_CONSTS, n[0]
            pool.sem_inc(rows_free, 1)

            pool.wait_ge(amax_in, 1)
            pool.partition_all_reduce(amax_all[:], amax[:], P, RMAX).then_inc(amax_out, 1)

            def step(j, jh, par):
                if live(j, 0, STEPS):
                    pool.wait_ge(ve1_ready, j + 1)
                    if late(j, 1):
                        pool.wait_ge(xn_ready, G * j)
                    pool.tensor_tensor(r1[:], ve1[:], nhalf[:, 0:G], ALU.pow).then_inc(r1_ready, 1)
                if live(j, 1, STEPS):
                    pool.wait_ge(ve2_ready, j)
                    if late(j, 2):
                        pool.wait_ge(xt_ready, (G + 1) * (j - 1))
                    pool.tensor_tensor(r2[:].rearrange("p a g -> p (a g)"), ve2[:].rearrange("p a g -> p (a g)"),
                                       nhalf[:], ALU.pow).then_inc(r2_ready, 1)
                if live(j, 2, STEPS):
                    wait_alone(pool, pos_ready, j - 1)
                    for g in range(G):
                        pool.indirect_dma_start(rows[:, :], bass.IndirectOffsetOnAxis(ap=pos[:, par, g:g + 1], axis=0),
                                                SR[:, par, g, :], None).then_inc(scattered[par], 16)
                    pool.wait_ge(scattered[par], 16 * G * jh)
                    pool.sem_inc(rows_free, 1)

            stage_a(step)

            def store(t, th, q):
                if live(t, 0, TILES):
                    wait_alone(pool, o_ready, t + 1)
                    pool.indirect_dma_start(
                        out[:, :], bass.IndirectOffsetOnAxis(ap=RC[:, q, TOK:TOK + 1].bitcast(I32), axis=0),
                        o[:, q, :], None, bounds_check=TOKENS - 1, oob_is_err=False).then_inc(stored[q], 16)

            stage_b(pool, store, TILES)

        @block.scalar
        def _(act):
            act.dma_start(wmsg[:], W_msg).then_inc(gnn_w, 16)
            act.dma_start(wupd[:], W_upd).then_inc(gnn_w, 16)
            act.dma_start(wr[:], Wr).then_inc(gnn_w, 16)
            act.dma_start(brb[:], br.rearrange("(o e) -> o e", o=1).partition_broadcast(P)).then_inc(gnn_w, 16)
            act.dma_start(b2row[:], b2.rearrange("(o e) d -> o e d", o=1).partition_broadcast(2)).then_inc(gnn_w, 16)
            for g in range(HG):
                act.dma_start(bias_row[:, g, :], bias.rearrange("(o d) -> o d", o=1)).then_inc(gnn_w, 16)
            act.dma_start(small_rows[0:E, :], ln_g).then_inc(ffn_w, 16)
            act.dma_start(small_rows[E:2 * E, :], ln_b).then_inc(ffn_w, 16)
            act.dma_start(small_rows[2 * E:, :], b1.rearrange("e (c p) -> (e c) p", p=P)).then_inc(ffn_w, 16)
            act.dma_start(w1f[:], W1.rearrange("e d h -> d e h")).then_inc(ffn_w, 16)
            for e in range(2):
                act.dma_start(w2f[:, e * 4:(e + 1) * 4], W2[e * 4:(e + 1) * 4].rearrange("e (c p) d -> p e c d", p=P))\
                    .then_inc(ffn_w, 16)

            def step(j, jh, par):
                if live(j, 2, STEPS):
                    act.wait_ge(gap_ready, j - 1)
                    nc.scalar.activation(rt[:, 7], rt[:, 6], ACT.Exp).then_inc(ex_ready, 1)
                if live(j, 0, STEPS):
                    act.wait_ge(adj_in[par], 16 * (jh + 1))
                    if late(j, 1):
                        act.wait_ge(ta_done, 2 * j)
                    nc.scalar.activation(AF[:], ADJ[:, par], ACT.Copy).then_inc(adj_f32, 1)
                    for h in range(2):
                        act.wait_ge(ta_done, 2 * j + h + 1)
                        if late(j, 1):
                            act.wait_ge(s2_done, 2 * (j - 1) + h + 1)
                        nc.scalar.activation(XNT[:, h], bank[0][:], ACT.Copy).then_inc(xnt_ready, 1)
                        nc.scalar.activation(AGT[:, h], bank[1][:], ACT.Copy).then_inc(xnt_ready, 1)
                    for h in range(2):
                        act.wait_ge(s2_done, 2 * j + h + 1)
                        if late(j, 1):
                            act.wait_ge(msg_used, HG * (2 * (j - 1) + h + 1))
                        nc.scalar.activation(U[:, h].rearrange("p g d -> p (g d)"), bank[2][:], ACT.Copy)\
                            .then_inc(u_ready, 1)
                if live(j, 1, STEPS):
                    for h in range(2):
                        act.wait_ge(xt_done, 2 * (j - 1) + h + 1)
                        if late(j, 2):
                            act.wait_ge(lg_done, 2 * (j - 2) + h + 1)
                        nc.scalar.activation(XTT[:, h], bank[0][:], ACT.Copy).then_inc(xtt_ready, 1)

            stage_a(step)

            def tile(t, th, q):
                def high(t, q):
                    act.wait_ge(xtb_done, t + 1)
                    nc.scalar.activation(xh[:, q], bank[6 + q % 2][:, 0:P], ACT.Copy).then_inc(xh_ready, 1)

                def gelu(t, q, k, ex):
                    u = 2 * t + k
                    z = 2 * (q % 2) + k
                    wait_alone(act, z_done, u + 1)
                    for c in range(C):
                        nc.scalar.activation(gl[:, z, c * P:(c + 1) * P], bank[z][:, c * P:(c + 1) * P], ACT.Gelu,
                                             bias=b1c[c][:, bass.ds(ex, 1)], scale=sc[:, 2:3])\
                            .then_inc(g_ready, 1)

                if isinstance(t, int) and t == 0:
                    act.wait_ge(weights_ready, 1)
                    act.wait_ge(tab_ready, 7)
                    high(0, 0)
                if live(t, -1, TILES):
                    high(t + 1, (q + 1) % 4)
                if live(t, 0, TILES):
                    ex = load_experts(act, t, 2)
                    for c in range(C):
                        for k in range(2):
                            act.lower_ap(b1c[c][:, bass.ds(ex[k], 1)])
                    gelu(t, q, 0, ex[0])
                if live(t, 0, TILES):
                    gelu(t, q, 1, ex[1])

            stage_b(act, tile, TILES)

        @block.tensor
        def _(pe):
            mm = nc.tensor.matmul
            pe.wait_ge(consts, N_CONSTS)
            pe.wait_ge(ffn_w, 16 * N_FFN_W)
            ns = 2 * E + E * C
            nc.tensor.transpose(bank[7][:, 0:ns], small_rows[:, :], ident[0:ns, 0:ns]).then_inc(setup_pe, 1)
            pe.wait_ge(dve, 1)
            for e in range(E):
                for c in range(C):
                    mm(bank[6][:, c * E + e:c * E + e + 1], w1f[:, e, c * P:(c + 1) * P], small_cols[:, E + e:E + e + 1],
                       start=True, stop=True).then_inc(setup_pe, 1)
            pe.wait_ge(gnn_w, 16 * N_GNN_W)

            def step(j, jh, par):
                if live(j, 2, STEPS):
                    pe.wait_ge(oh_ready, j - 1)
                    if late(j, 3):
                        pe.wait_ge(pos_ready, j - 2)
                    mm(bank[7][:, 0:G * NP], tri[:], oh[:].rearrange("p g n -> p (g n)"), start=True, stop=False)
                    mm(bank[7][:, 0:G * NP], ones_b[:], pre[:, 0:G].rearrange("p g n -> p (g n)"), start=False,
                       stop=True).then_inc(rank_done, 1)
                if live(j, 0, STEPS):
                    for h in range(2):
                        pe.wait_ge(xn_ready, G * j + HG * (h + 1))
                        if h == 0:
                            pe.wait_ge(adj_f32, j + 1)
                            if late(j, 1):
                                pe.wait_ge(deg_used, j)
                            if late(j, 2):
                                pe.wait_ge(xtt_ready, 2 * (j - 1))
                        if h == 1 or late(j, 1):
                            pe.wait_ge(xnt_ready, 2 * (2 * j + h))
                        for g in range(HG):
                            gg = h * HG + g
                            nc.tensor.transpose(bank[0][:, g * P:(g + 1) * P], XN[:, gg, :], ident[:])
                            mm(bank[1][:, g * P:(g + 1) * P], XN[:, gg, :], AF[:, gg, :], start=True, stop=True)
                            last = mm(bank[5][:, gg:gg + 1], AF[:, gg, :], ones_f[:], start=True, stop=True)
                        last.then_inc(ta_done, 1)
                    for h in range(2):
                        pe.wait_ge(xnt_ready, 2 * (2 * j + h + 1))
                        if h == 1 or late(j, 1):
                            pe.wait_ge(u_ready, 2 * j + h)
                        if late(j, 1):
                            pe.wait_ge(msg_used, HG * (2 * (j - 1) + h + 1))
                        mm(bank[2][:], ones_row[:], bias_row[:].rearrange("o g d -> o (g d)"), start=True, stop=False)
                        for g in range(HG):
                            mm(bank[2][:, g * P:(g + 1) * P], XNT[:, h, g * P:(g + 1) * P], wupd[:], start=False,
                               stop=(g == HG - 1))
                        for g in range(HG):
                            last = mm(bank[3 + h][:, g * P:(g + 1) * P], AGT[:, h, g * P:(g + 1) * P], wmsg[:],
                                      start=True, stop=True)
                        last.then_inc(s2_done, 1)
                if live(j, 1, STEPS):
                    for h in range(2):
                        pe.wait_ge(xt_ready, (G + 1) * (j - 1) + HG * (h + 1))
                        if h == 0:
                            if live(j, 0, STEPS):
                                pe.wait_ge(xnt_ready, 2 * (2 * j + 2))
                            elif late(j, 2):
                                pe.wait_ge(xtt_ready, 2 * (j - 1))
                        else:
                            pe.wait_ge(xtt_ready, 2 * (j - 1) + 1)
                        for g in range(HG):
                            last = nc.tensor.transpose(bank[0][:, g * P:(g + 1) * P], XT[:, h * HG + g, :], ident[:])
                        last.then_inc(xt_done, 1)
                    for h in range(2):
                        pe.wait_ge(xtt_ready, 2 * (j - 1) + h + 1)
                        if late(j, 2):
                            pe.wait_ge(lg_used, j - 1)
                        for g in range(HG):
                            gg = h * HG + g
                            last = mm(bank[6][:, gg * E:(gg + 1) * E], XTT[:, h, g * P:(g + 1) * P], wr[:],
                                      start=True, stop=True)
                        last.then_inc(lg_done, 1)

            stage_a(step)
            pe.wait_ge(pos_ready, STEPS)
            mm(bank[7][:, 0:NP], ones_b[:], pre[:, 0], start=True, stop=True).then_inc(total_done, 1)
            pe.wait_ge(fld_ready, 1)
            for f in range(3):
                mm(bank[5][0:1, f * P:(f + 1) * P], fld[:, f:f + 1], ident[:], start=True, stop=True)\
                    .then_inc(fld_row, 1)

            pe.wait_ge(weights_ready, 1)
            pe.wait_ge(tab_ready, 7)

            def turn(t, q):
                pe.wait_ge(xs_ready, t + 1)
                nc.tensor.transpose(bank[6 + q % 2][:, 0:P], xs[:, q % 2, :], ident[:]).then_inc(xtb_done, 1)

            def up(t, q, k, ex):
                z = 2 * (q % 2) + k
                if k == 0:
                    pe.wait_ge(xl_ready, t + 1)
                for c in range(C):
                    zz = bank[z][:, c * P:(c + 1) * P]
                    wh = w1h[c][:, bass.ds(ex, 1), :]
                    mm(zz, wh, xh[:, q], start=True, stop=False)
                    mm(zz, wh, xl[:, q], start=False, stop=False)
                    last = mm(zz, w1l[c][:, bass.ds(ex, 1), :], xh[:, q], start=False, stop=True)
                last.then_inc(z_done, 1)

            def down(t, q, k, ex):
                u, z = 2 * t + k, 2 * (q % 2) + k
                pe.wait_ge(h_ready, 2 * (u + 1))
                y = bank[4 + q % 2][:, k * D:(k + 1) * D]
                mm(y, ones2[:], b2t[:, bass.ds(ex, 1), :], start=True, stop=False)
                for c in range(C):
                    mm(y, hh[:, z, c * P:(c + 1) * P], w2h[c][:, bass.ds(ex, 1), :], start=False, stop=False)
                    mm(y, hh[:, z, c * P:(c + 1) * P], w2l[c][:, bass.ds(ex, 1), :], start=False, stop=False)
                    last = mm(y, hl[:, z, c * P:(c + 1) * P], w2h[c][:, bass.ds(ex, 1), :], start=False,
                              stop=(c == C - 1))
                last.then_inc(y_done, 1)

            def addresses_up(ex):
                for c in range(C):
                    for w in (w1h, w1l):
                        pe.lower_ap(w[c][:, bass.ds(ex, 1), :], for_matmul_weights=True)

            def addresses_down(ex):
                pe.lower_ap(b2t[:, bass.ds(ex, 1), :])
                for c in range(C):
                    for w in (w2h, w2l):
                        pe.lower_ap(w[c][:, bass.ds(ex, 1), :])

            def tile(t, th, q):
                if isinstance(t, int) and t == 0:
                    turn(0, 0)
                    turn(1, 1)
                ex = load_experts(pe, t, 4)
                if live(t, 0, TILES):
                    addresses_up(ex[0])
                    up(t, q, 0, ex[0])
                if live(t, 2, TILES):
                    addresses_down(ex[2])
                    down(t - 2, (q + 2) % 4, 1, ex[2])
                if live(t, 0, TILES):
                    addresses_up(ex[1])
                    up(t, q, 1, ex[1])
                if live(t, 1, TILES):
                    addresses_down(ex[3])
                    down(t - 1, (q + 3) % 4, 0, ex[3])
                if live(t, -2, TILES):
                    turn(t + 2, (q + 2) % 4)

            stage_b(pe, tile, TILES + 2)

        @block.vector
        def _(v):
            ts, tt, stt = nc.vector.tensor_scalar, nc.vector.tensor_tensor, nc.vector.scalar_tensor_tensor
            done = Done(v, dve)

            v.wait_ge(consts, N_CONSTS)
            v.wait_ge(setup_pe, 1)
            cols = done(nc.vector.tensor_copy(small_cols[:], bank[7][:, 0:2 * E + E * C]))
            v.wait_ge(ffn_w, 16 * N_FFN_W)
            v.wait_ge(gnn_w, 16 * N_GNN_W)
            m = done(nc.vector.tensor_reduce(amw[:], w1f[:], AX.X, ALU.max, apply_absolute_value=True))
            done(nc.vector.tensor_reduce(amax[:, 1:2], w2f[:].rearrange("p e c d -> p (e c d)"), AX.X, ALU.max,
                                         apply_absolute_value=True))
            done(nc.vector.tensor_reduce(amax[0:2, 3:4], b2row[:].rearrange("p e d -> p (e d)"), AX.X, ALU.max,
                                         apply_absolute_value=True))
            v.wait_ge(setup_pe, 1 + E * C)
            m = done(tt(b1s[:], bank[6][:, 0:E * C].rearrange("p (c e) -> p c e", c=C),
                        small_cols[:, 2 * E:].rearrange("p (e c) -> p c e", c=C), ALU.add))
            done.wait(m)
            for c in range(C):
                done(nc.vector.tensor_copy(b1c[c][:], b1s[:, c]))
            done(nc.vector.tensor_reduce(amax[:, 2:3], b1s[:].rearrange("p c e -> p (c e)"), AX.X, ALU.max, apply_absolute_value=True))
            m = done(tt(amw[:], amw[:], small_cols[:, 0:E], ALU.mult))
            done.wait(m)
            nc.vector.tensor_reduce(amax[:, 0:1], amw[:], AX.X, ALU.max, apply_absolute_value=True)\
                .then_inc(amax_in, 1)
            v.wait_ge(amax_out, 1)
            m = done(ts(sc[:, 0:1], amax_all[:, 0:1], 1e-30, None, ALU.max))
            m = done(tt(sc[:, 1:2], amax_all[:, 1:2], amax_all[:, 3:4], ALU.max))
            done.wait(m)
            done(ts(sc[:, 1:2], sc[:, 1:2], 1e-30, None, ALU.max))
            m = done(stt(sc[:, 7:8], sc[:, 0:1], float(D), amax_all[:, 2:3], ALU.mult, ALU.add))
            done.wait(m)
            m = done(ts(sc[:, 8:9], sc[:, 7:8], 1.0, None, ALU.max))
            done.wait(m)
            done(ts(sc[:, 9:10].bitcast(I32), sc[:, 0:1].bitcast(I32), 0x7F800000, None, ALU.bitwise_and))
            done(ts(sc[:, 10:11].bitcast(I32), sc[:, 1:2].bitcast(I32), 0x7F800000, None, ALU.bitwise_and))
            m = done(ts(sc[:, 11:12].bitcast(I32), sc[:, 8:9].bitcast(I32), 0x7F800000, None, ALU.bitwise_and))
            done.wait(m)
            m = done(nc.vector.reciprocal(sc[:, 12:15], sc[:, 9:12]))
            done.wait(m)
            done(ts(sc[:, 2:3], sc[:, 9:10], 2.0 ** -9, None, ALU.mult))
            done(ts(sc[:, 3:4], sc[:, 12:13], 2.0 ** 9, None, ALU.mult))
            done(ts(sc[:, 4:5], sc[:, 13:14], 2.0 ** 9, None, ALU.mult))
            done(ts(sc[:, 5:6], sc[:, 14:15], 2.0 ** 14, None, ALU.mult))
            m = done(tt(sc[:, 6:7], sc[:, 10:11], sc[:, 11:12], ALU.mult))
            done.wait(m)
            done(ts(sc[:, 6:7], sc[:, 6:7], 2.0 ** -23, None, ALU.mult))
            done(ts(gsc[:], small_cols[:, 0:E], sc[:, 3:4], None, ALU.mult))
            done(ts(b2sc[:], b2row[:], sc[0:2, 4:5], None, ALU.mult))
            m = done(ts(ones2[0:2, :], ident[0:2, :], 0.0, sc[0:2, 5:6], ALU.mult, ALU.add))
            done.wait(m)
            for e in range(E):
                m = done(ts(w1f[:, e], w1f[:, e], gsc[:, e:e + 1], None, ALU.mult))
            done(nc.vector.tensor_copy(b2hi[:], b2sc[:]))
            done.wait(m)
            for c in range(C):
                done(nc.vector.tensor_copy(w1h[c][:], w1f[:, :, c * P:(c + 1) * P]))
                m = done(ts(w2h[c][:], w2f[:, :, c], sc[:, 4:5], None, ALU.mult))
            done.wait(m)
            for c in range(C):
                done(tt(w1l[c][:], w1f[:, :, c * P:(c + 1) * P], w1h[c][:], ALU.subtract))
                done(stt(w2l[c][:], w2f[:, :, c], sc[:, 4:5], w2h[c][:], ALU.mult, ALU.subtract))
            m = done(tt(b2hi32[:], b2sc[:], b2hi[:], ALU.subtract))
            done.wait(m)
            m = done(tt(b2hi32[:], b2hi32[:], b2hi[:], ALU.subtract))
            done.wait(m)
            stt(b2t[0:2].rearrange("p e d -> p (e d)"), b2hi32[:].rearrange("p e d -> p (e d)"), halfsel[:, 0:1],
                b2hi[:].rearrange("p e d -> p (e d)"), ALU.mult, ALU.add).then_inc(weights_ready, 1)

            l, q1, o1_, q2 = (L[:, i] for i in range(4))
            m1, k1, m2, k2, hi, key, gap, ex, den, w1_, w2_, sw, dw, sdw, lo = (rt[:, i] for i in range(15))
            shape = [P, G, E]

            def wide(a):
                return a.unsqueeze(2).to_broadcast(shape)

            def step(j, jh, par):
                if live(j, 2, STEPS):
                    v.wait_ge(lg_done, 2 * (j - 1))
                    tt(l, bank[6][:, 0:G * E].rearrange("p (g e) -> p g e", g=G),
                       brb[:].unsqueeze(1).to_broadcast(shape), ALU.add).then_inc(lg_used, 1)
                    v.wait_ge(lg_used, j - 1)
                    m = done(nc.vector.tensor_reduce(m1, l, AX.X, ALU.max))
                    done.wait(m)
                    m = done(tt(q1, l, wide(m1), ALU.is_equal))
                    done.wait(m)
                    m = done(tt(q1, q1, rev[:], ALU.mult))
                    done.wait(m)
                    m = done(nc.vector.tensor_reduce(k1, q1, AX.X, ALU.max))
                    done.wait(m)
                    m = done(tt(o1_, rev[:], wide(k1), ALU.is_equal))
                    done.wait(m)
                    m = done(stt(q2, o1_, BIG, l, ALU.mult, ALU.add))
                    done.wait(m)
                    m = done(nc.vector.tensor_reduce(m2, q2, AX.X, ALU.max))
                    done.wait(m)
                    tt(gap, m2, m1, ALU.subtract).then_inc(gap_ready, 1)
                    m = done(tt(q1, q2, wide(m2), ALU.is_equal))
                    done.wait(m)
                    m = done(tt(q1, q1, rev[:], ALU.mult))
                    done.wait(m)
                    m = done(nc.vector.tensor_reduce(k2, q1, AX.X, ALU.max))
                    done.wait(m)
                    done(tt(sw, k2, k1, ALU.is_gt))
                    done(tt(lo, k1, k2, ALU.min))
                    m = done(tt(hi, k1, k2, ALU.max))
                    done.wait(m)
                    m = done(stt(key, hi, float(E), lo, ALU.mult, ALU.add))
                    done.wait(m)
                    m = done(tt(oh[:], keys[:], key.unsqueeze(2).to_broadcast([P, G, NP]), ALU.is_equal))
                    done.wait(m)
                    for g in range(G):
                        i_ = tt(pre[:, g + 1], pre[:, g], oh[:, g], ALU.add)
                        if g < G - 1:
                            m = done(i_)
                            done.wait(m)
                        else:
                            i_.then_inc(oh_ready, 1)
                if live(j, 0, STEPS):
                    v.wait_ge(x_in[par], 16 * (jh + 1))
                    for g in range(G):
                        m = done(nc.vector.bn_stats(st1[:, g], X[:, par, g]))
                    wait_alone(v, dve, m)
                    for g in range(G):
                        m = done(nc.vector.bn_aggr(mv1[:, g], st1[:, g]))
                    done.wait(m)
                    if late(j, 1):
                        v.wait_ge(r1_ready, j)
                    ts(ve1[:], mv1[:, :, 1], EPS, None, ALU.add).then_inc(ve1_ready, 1)
                if live(j, 1, STEPS):
                    p1 = 1 - par
                    v.wait_ge(ta_done, 2 * j)
                    m = done(ts(dg[:, 0], bank[5][:, 0:G], 1.0, None, ALU.max))
                    done.wait(m)
                    m = done(nc.vector.reciprocal(dg[:, 1], dg[:, 0]))
                    done.wait(m)
                    stt(dg[:, 2], bank[5][:, 0:G], 0.0, dg[:, 1], ALU.is_gt, ALU.mult).then_inc(deg_used, 1)
                    v.wait_ge(deg_used, j)
                    for h in range(2):
                        v.wait_ge(s2_done, 2 * (j - 1) + h + 1)
                        v.wait_ge(u_ready, 2 * (j - 1) + h + 1)
                        for g in range(HG):
                            gg = h * HG + g
                            stt(T[:, h, g], bank[3 + h][:, g * P:(g + 1) * P], dg[:, 2, gg:gg + 1], U[:, h, g],
                                ALU.mult, ALU.add).then_inc(msg_used, 1)
                    for h in range(2):
                        v.wait_ge(msg_used, HG * (2 * (j - 1) + h + 1))
                        if late(j, 2):
                            v.wait_ge(rows_free, j - 1)
                        stt(SR[:, p1, h * HG:(h + 1) * HG, 0:D], T[:, h], 0.0, X[:, p1, h * HG:(h + 1) * HG],
                            ALU.max, ALU.add).then_inc(x2_ready, 1)
                    v.wait_ge(x2_ready, 2 * j)
                    for g in range(G):
                        m = done(nc.vector.bn_stats(st2[:, g], SR[:, p1, g, 0:D]))
                    wait_alone(v, dve, m)
                    for g in range(G):
                        m = done(nc.vector.bn_aggr(mv2[:, g], st2[:, g]))
                    done.wait(m)
                    if late(j, 2):
                        v.wait_ge(r2_ready, j - 1)
                    m = done(ts(ve2[:, 0], mv2[:, :, 1], EPS, None, ALU.add))
                    done.wait(m)
                    stt(ve2[:, 1], ve2[:, 0], EPS, mv2[:, :, 1], ALU.mult, ALU.add).then_inc(ve2_ready, 1)
                    done(nc.vector.tensor_copy(SR[:, p1, :, MU], mv2[:, :, 0]))
                if live(j, 0, STEPS):
                    v.wait_ge(r1_ready, j + 1)
                    if late(j, 1):
                        v.wait_ge(ta_done, 2 * j)
                    for g in range(G):
                        ts(XN[:, g], X[:, par, g], mv1[:, g, 0:1], r1[:, g:g + 1], ALU.subtract, ALU.mult)\
                            .then_inc(xn_ready, 1)
                if live(j, 1, STEPS):
                    p1 = 1 - par
                    v.wait_ge(r2_ready, j)
                    if late(j, 2):
                        v.wait_ge(xt_done, 2 * (j - 1))
                    for g in range(G):
                        ts(XT[:, g], SR[:, p1, g, 0:D], mv2[:, g, 0:1], r2[:, 0, g:g + 1], ALU.subtract, ALU.mult)\
                            .then_inc(xt_ready, 1)
                    nc.vector.tensor_copy(SR[:, p1, :, RS], r2[:, 1]).then_inc(xt_ready, 1)
                if live(j, 2, STEPS):
                    v.wait_ge(ex_ready, j - 1)
                    m = done(ts(den, ex, 1.0, None, ALU.add))
                    done.wait(m)
                    m = done(nc.vector.reciprocal(w1_, den))
                    done.wait(m)
                    m = done(ts(w1_, w1_, sc[:, 6:7], None, ALU.mult))
                    done.wait(m)
                    m = done(tt(w2_, ex, w1_, ALU.mult))
                    done.wait(m)
                    m = done(tt(dw, w2_, w1_, ALU.subtract))
                    done.wait(m)
                    m = done(tt(sdw, sw, dw, ALU.mult))
                    done.wait(m)
                    done(tt(SR[:, par, :, WA], w1_, sdw, ALU.add))
                    done(tt(SR[:, par, :, WB], w2_, sdw, ALU.subtract))
                    done(nc.vector.tensor_copy(SR[:, par, :, TOK].bitcast(I32), tok[:]))
                    v.wait_ge(rank_done, j - 1)
                    m = done(nc.vector.tensor_copy(pre[:, 0], pre[:, G]))
                    m = done(tt(rk[:], bank[7][:, 0:G * NP].rearrange("p (g n) -> p g n", g=G), rowb[:], ALU.add))
                    done.wait(m)
                    m = done(tt(rk[:], rk[:], oh[:], ALU.mult))
                    m = done(ts(tok[:], tok[:], float(G * N), None, ALU.add))
                    done.wait(m)
                    with nc.allow_low_precision(reason="sums of whole numbers below 2**24"):
                        nc.vector.tensor_reduce(pos[:, par], rk[:], AX.X, ALU.add).then_inc(pos_ready, 1)

            stage_a(step)

            v.wait_ge(pos_ready, STEPS)
            done(nc.vector.memset(fld[:, 3:4], 0.0))
            v.wait_ge(total_done, 1)
            done(nc.vector.tensor_copy(cntf[:], bank[7][:, 0:NP]))
            m = done(ts(cnti[:], bank[7][:, 0:NP], float(P - 1), None, ALU.add))
            done.wait(m)
            tt(fill[:], cntf[0:1], rowb[0:1, 0], ALU.add).then_inc(fill_ready, 1)
            m = done(ts(cnti[:], cnti[:], 7, None, ALU.logical_shift_right))
            done.wait(m)
            m = done(nc.vector.tensor_copy(ntf[:], cnti[:]))
            done.wait(m)
            m = done(nc.vector.tensor_copy(inc[:, 0], ntf[:]))
            done.wait(m)
            a, s = 0, 1
            while s < NP:
                done(tt(inc[:, 1 - a, s:], inc[:, a, s:], inc[:, a, :NP - s], ALU.add))
                m = done(nc.vector.tensor_copy(inc[:, 1 - a, :s], inc[:, a, :s]))
                done.wait(m)
                a, s = 1 - a, 2 * s
            last = inc[:, a]
            m = done(tt(tw[:, 0], last, ntf[:], ALU.subtract))
            done.wait(m)
            done(ts(tw[:, 1], tw[:, 0], tcol[:, 0:1], None, ALU.is_le))
            m = done(ts(tw[:, 2], last, tcol[:, 0:1], None, ALU.is_gt))
            done.wait(m)
            m = done(tt(tw[:, 1], tw[:, 1], tw[:, 2], ALU.mult))
            m = done(ts(tw[:, 3], tw[:, 0], tcol[:, 0:1], -float(P), ALU.subtract, ALU.mult))
            done.wait(m)
            m = done(tt(tw[:, 3], tw[:, 3], rowb[:, 0], ALU.add))
            done.wait(m)
            m = done(ts(tw[:, 3], tw[:, 3], float(PAD_SEG), None, ALU.subtract))
            done.wait(m)
            m = done(tt(tw[:, 3], tw[:, 3], tw[:, 1], ALU.mult))
            done(tt(tw[:, 0], exp_a[:], tw[:, 1], ALU.mult))
            m = done(tt(tw[:, 2], exp_b[:], tw[:, 1], ALU.mult))
            done.wait(m)
            done(nc.vector.tensor_reduce(fld[:, 0:1], tw[:, 0], AX.X, ALU.add))
            done(nc.vector.tensor_reduce(fld[:, 1:2], tw[:, 2], AX.X, ALU.add))
            m = done(nc.vector.tensor_reduce(fld[:, 2:3], tw[:, 3], AX.X, ALU.add))
            done.wait(m)
            ts(fld[:, 2:3], fld[:, 2:3], float(PAD_SEG), None, ALU.add).then_inc(fld_ready, 1)
            v.wait_ge(fld_row, 3)
            for k in range(2):
                nc.vector.tensor_copy(experts[:, :, k], bank[5][0:1, k * P:(k + 1) * P]).then_inc(tab_ready, 1)
                back = 1 if k == 0 else 2
                nc.vector.tensor_copy(experts[:, back:, 3 - k], bank[5][0:1, k * P:(k + 1) * P - back])\
                    .then_inc(tab_ready, 1)
            nc.vector.memset(experts[:, 0, 3:4], 0).then_inc(tab_ready, 1)
            nc.vector.memset(experts[:, 0:2, 2:3], 0).then_inc(tab_ready, 1)
            nc.vector.tensor_copy(tile_row[:], bank[5][0:1, 2 * P:3 * P]).then_inc(tab_ready, 1)

            def normal(t, th, q):
                v.wait_ge(ra_in[q], 16 * (th + 1))
                ts(xs[:, q % 2], RA[:, q, 0:D], RA[:, q, MU:MU + 1], RA[:, q, RS:RS + 1], ALU.subtract, ALU.mult)\
                    .then_inc(xs_ready, 1)

            def low(t, q):
                v.wait_ge(xh_ready, t + 1)
                tt(xl[:, q], bank[6 + q % 2][:, 0:P], xh[:, q], ALU.subtract).then_inc(xl_ready, 1)

            def high_half(t, q, k):
                u, z = 2 * t + k, 2 * (q % 2) + k
                v.wait_ge(g_ready, C * (u + 1))
                ts(hh[:, z], gl[:, z], sc[:, 5:6], None, ALU.mult).then_inc(h_ready, 1)

            def low_half(t, q, k):
                u, z = 2 * t + k, 2 * (q % 2) + k
                v.wait_ge(h_ready, 2 * u + 1)
                stt(hl[:, z], gl[:, z], sc[:, 5:6], hh[:, z], ALU.mult, ALU.subtract).then_inc(h_ready, 1)

            def combine_a(t, th, q):
                v.wait_ge(y_done, 2 * (t + 1))
                v.wait_ge(rc_in[q], 16 * (th + 1))
                done(stt(o1[:, q % 2], bank[4 + q % 2][:, 0:D], RC[:, q, WA:WA + 1], RC[:, q, 0:D], ALU.mult,
                         ALU.add))

            def combine_b(t, th, q, a_done):
                done.wait(a_done)
                stt(o[:, q], bank[4 + q % 2][:, D:2 * D], RC[:, q, WB:WB + 1], o1[:, q % 2], ALU.mult, ALU.add)\
                    .then_inc(o_ready, 1)

            def tile(t, th, q):
                _, th2, q2 = near(t, th, q, -2)
                if isinstance(t, int) and t == 0:
                    normal(0, 0, 0)
                    normal(1, 0, 1)
                    low(0, 0)
                    normal(2, 0, 2)
                if live(t, -1, TILES):
                    low(t + 1, (q + 1) % 4)
                if live(t, 0, TILES):
                    high_half(t, q, 0)
                if live(t, 2, TILES):
                    combine_a(t - 2, th2, q2)
                    a_done = done.base + done.n
                if live(t, -3, TILES):
                    normal(*near(t, th, q, 3))
                if live(t, 2, TILES):
                    combine_b(t - 2, th2, q2, a_done)
                if live(t, 0, TILES):
                    low_half(t, q, 0)
                    high_half(t, q, 1)
                    low_half(t, q, 1)

            b0 = [done.base + done.n, 0]

            def rebase_b(i):
                done.rebase(b0[0] + 4 * i - 2)

            stage_b(v, tile, TILES + 2, rebase_b)


N_CONSTS = 12 + 3 + 3 * (E - 1) + 5
RMAX = bass.bass_isa.ReduceOp.max

_INS = ["x", "adj", "L0_gnn_W_msg", "L0_gnn_W_upd", "L0_gnn_bias", "L0_ffn_Wr", "L0_ffn_br", "L0_ffn_ln_g",
        "L0_ffn_ln_b", "L0_ffn_W1", "L0_ffn_b1", "L0_ffn_W2", "L0_ffn_b2"]


def kernel(**inputs):
    import numpy as _np
    import concourse.bacc as _bacc
    from concourse.bass_utils import run_bass_kernel_spmd as _run

    nc = _bacc.Bacc("TRN2", target_bir_lowering=False, num_devices=1)
    arrays, args = {}, []
    for name in _INS:
        a = _np.ascontiguousarray(inputs[name])
        arrays[f"in_{name}"] = a
        args.append(nc.dram_tensor(f"in_{name}", a.shape, mybir.dt.from_np(a.dtype), kind="ExternalInput").ap())
    out = nc.dram_tensor("out_rows", (TOKENS, D), F32, kind="ExternalOutput").ap()
    moe_gnn(nc, *args, out)
    r = _run(nc, [arrays], core_ids=[0])
    return r.results[0]["out_rows"].reshape(B, N, D)
```

```python
import numpy as np
import concourse.bass as bass
from concourse import mybir
from contextlib import ExitStack

F32, F16, BF16, I32 = mybir.dt.float32, mybir.dt.float16, mybir.dt.bfloat16, mybir.dt.int32
ALU = mybir.AluOpType
ACT = mybir.ActivationFunctionType
AX = mybir.AxisListType

P = 128
B, N, D = 64, 128, 128
E, H = 8, 512
C = H // P
TOKENS = B * N
EPS = 1e-5

G = 8
HG = G // 2
STEPS = B // G

PAIRS = [(a, b) for a in range(E) for b in range(a + 1, E)]
NP = len(PAIRS)
SEG = TOKENS + P
PAD_SEG = NP * SEG
TILES = TOKENS // P + NP - 1

RING = 8

MU, RS, WA, WB, TOK, ROW = D, D + 1, D + 2, D + 3, D + 4, D + 8

BIG = -3.0e38


class Done:

    def __init__(self, engine, sem):
        self.engine, self.sem, self.base, self.n = engine, sem, 0, 0

    def __call__(self, instruction):
        instruction.then_inc(self.sem, 1)
        self.n += 1
        return self.base + self.n

    def wait(self, mark):
        self.engine.wait_ge(self.sem, mark)

    def rebase(self, base):
        self.base, self.n = base, 0


def moe_gnn(nc, x, adj, W_msg, W_upd, bias, Wr, br, ln_g, ln_b, W1, b1, W2, b2, out):
    ctx = ExitStack()
    with ctx:
        def sb(name, shape, dt):
            return ctx.enter_context(nc.sbuf_tensor(name, shape, dt))

        def sem(name):
            return ctx.enter_context(nc.semaphore(name))

        rows = nc.dram_tensor("rows", (PAD_SEG + P, ROW), F32, kind="Internal").ap()

        ident = sb("ident", [P, P], F32)
        tri = sb("tri", [P, P], BF16)
        ones_b = sb("ones_b", [P, P], BF16)
        rev = sb("rev", [P, G, E], F32)
        keys = sb("keys", [P, G, NP], F32)
        rowb = sb("rowb", [P, G, NP], F32)
        exp_a = sb("exp_a", [P, NP], F32)
        exp_b = sb("exp_b", [P, NP], F32)
        tcol = sb("tcol", [P, 1], F32)
        tok = sb("tok", [P, G], F32)
        nhalf = sb("nhalf", [P, 2 * G], F32)
        warm = sb("warm", [P, 1], F32)
        padrow = sb("padrow", [P, ROW], F32)

        wr = sb("wr", [P, E], F32)
        brb = sb("brb", [P, E], F32)
        wgnn = sb("wgnn", [P, 2 * D], F32)
        bias_rows = sb("bias_rows", [3, 2, D], F32)
        bias_rest = sb("bias_rest", [3, 2, D], F32)
        bias_part = sb("bias_part", [3, 3, 2, D], BF16)
        bias3 = sb("bias3", [3, 2, D], BF16)
        sel3 = sb("sel3", [3, 3], F32)
        w1f = sb("w1f", [P, E, H], F32)
        w2f = sb("w2f", [P, E, C, D], F32)
        w1h = [sb(f"w1h{c}", [P, E, P], F16) for c in range(C)]
        w1l = [sb(f"w1l{c}", [P, E, P], F16) for c in range(C)]
        w2h = [sb(f"w2h{c}", [P, E, D], F16) for c in range(C)]
        w2l = [sb(f"w2l{c}", [P, E, D], F16) for c in range(C)]
        b1c = [sb(f"b1c{c}", [P, E], F32) for c in range(C)]
        small_rows = sb("small_rows", [2 * E + E * C, P], F32)
        small_cols = sb("small_cols", [P, 2 * E + E * C], F32)
        b2row = sb("b2row", [2, E, D], F32)
        b2s = sb("b2s", [E, D], F32)
        b2sc = sb("b2sc", [2, E, D], F32)
        b2hi = sb("b2hi", [2, E, D], F16)
        b2t = sb("b2t", [P, E, D], F16)
        b2hi32 = sb("b2hi32", [2, E, D], F32)
        halfsel = sb("halfsel", [2, 1], F32)
        ones2 = sb("ones2", [P, P], F16)
        b1s = sb("b1s", [P, C, E], F32)
        gsc = sb("gsc", [P, E], F32)
        amax = sb("amax", [P, 4], F32)
        amax_all = sb("amax_all", [P, 4], F32)
        amw = sb("amw", [P, E], F32)
        sc = sb("sc", [P, 16], F32)

        X = sb("X", [P, 3, G, D], F32)
        ADJ = sb("ADJ", [P, 2, G, N], I32)
        AF = sb("AF", [P, 2, G, N], F32)
        XN = sb("XN", [P, 2, G, D], F32)
        XNT = sb("XNT", [P, 2, HG * P], F32)
        UH = sb("UH", [P, G, 2 * D + 1], F32)
        T = sb("T", [P, 2, HG, D], F32)
        SR = sb("SR", [P, 4, G, ROW], F32)
        XT = sb("XT", [P, G, D], F32)
        XTT = sb("XTT", [P, 2, HG * P], F32)
        st1 = sb("st1", [P, G, 6], F32)
        mv1 = sb("mv1", [P, G, 2], F32)
        ve1 = sb("ve1", [P, G], F32)
        nm1 = sb("nm1", [P, 2, G], F32)
        r1 = sb("r1", [P, G], F32)
        st2 = sb("st2", [P, G, 6], F32)
        mv2 = sb("mv2", [P, G, 2], F32)
        nm2 = sb("nm2", [P, 2, G], F32)
        ve2 = sb("ve2", [P, 2, G], F32)
        r2 = sb("r2", [P, 2, G], F32)
        dg = sb("dg", [P, 4, G], F32)
        L = sb("L", [P, 4, G, E], F32)
        rt = sb("rt", [P, 20, G], F32)
        oh = sb("oh", [P, G, NP], BF16)
        carry = sb("carry", [P, NP], BF16)
        csum = sb("csum", [P, NP], BF16)
        rk = sb("rk", [P, G, NP], F32)
        pos = sb("pos", [P, 2, G], I32)

        cntf = sb("cntf", [P, NP], F32)
        cnti = sb("cnti", [P, NP], I32)
        ntf = sb("ntf", [P, NP], F32)
        inc = sb("inc", [P, 2, NP], F32)
        tw = sb("tw", [P, 4, NP], F32)
        fld = sb("fld", [P, 4], F32)
        experts = sb("experts", [1, P, 4], I32)
        tile_row = sb("tile_row", [1, P], I32)
        fill = sb("fill", [1, NP], I32)

        R = sb("R", [P, RING, ROW], F32)
        xs = sb("xs", [P, 2, D], F32)
        xh = sb("xh", [P, RING, P], F16)
        xl = sb("xl", [P, RING, P], F16)
        gl = sb("gl", [P, 4, H], F32)
        hh = sb("hh", [P, 4, H], F16)
        hl = sb("hl", [P, 4, H], F16)
        o = sb("o", [P, RING, D], F32)
        o1 = sb("o1", [P, 2, D], F32)

        bank = [ctx.enter_context(nc.psum_tensor(f"bank{i}", [P, 512], F32)) for i in range(8)]

        consts = sem("consts")
        gnn_w = sem("gnn_w")
        ffn_w = sem("ffn_w")
        x_in = [sem(f"x_in{i}") for i in range(3)]
        adj_in = [sem(f"adj_in{i}") for i in range(2)]
        dve = sem("dve_done")
        setup_pe = sem("setup_pe")
        cols_ready, scales_ready = sem("cols_ready"), sem("scales_ready")
        w1_scaled, high_ready = sem("w1_scaled"), sem("high_ready")
        amax_in = sem("amax_in")
        amax_out = sem("amax_out")
        ve1_ready, r1_ready = sem("ve1_ready"), sem("r1_ready")
        ve2_ready, r2_ready = sem("ve2_ready"), sem("r2_ready")
        r2_used = sem("r2_used")
        xn_ready, xt_ready = sem("xn_ready"), sem("xt_ready")
        xnt_done, uh_done, msg_done = sem("xnt_done"), sem("uh_done"), sem("msg_done")
        xt_done, lg_done = sem("xtr_done"), sem("lg_done")
        adj_f32 = sem("adj_f32")
        xnt_ready, uh_ready, xtt_ready = sem("xnt_ready"), sem("uh_ready"), sem("xtt_ready")
        bias_ready = sem("bias_ready")
        deg_ready, msg_used, x2_ready = sem("deg_used"), sem("msg_used"), sem("x2_ready")
        lg_used, gap_ready, ex_ready = sem("lg_used"), sem("gap_ready"), sem("ex_ready")
        oh_ready, rank_done, pos_ready = sem("oh_ready"), sem("rank_done"), sem("pos_ready")
        scattered = [sem(f"scattered{i}") for i in range(4)]
        total_done, fld_ready, fld_row = sem("total_done"), sem("fld_ready"), sem("fld_row")
        tab_ready, fill_ready, padded = sem("tab_ready"), sem("fill_ready"), sem("padded")
        weights_ready = sem("weights_ready")
        r_in = [sem(f"r_in{i}") for i in range(RING)]
        xs_ready, xtb_done, xh_ready, xl_ready = sem("xs_ready"), sem("xtb_done"), sem("xh_ready"), sem("xl_ready")
        z_done, g_ready, h_ready, y_done = sem("z_done"), sem("g_ready"), sem("h_ready"), sem("y_done")
        o_ready = sem("o_ready")
        passed = sem("passed")
        stored = [sem(f"stored{i}") for i in range(RING)]

        block = ctx.enter_context(nc.Block())

        N_GNN_W = 8
        N_FFN_W = 6

        def wait_alone(eng, semaphore, value):
            eng.wait_ge(semaphore, value)
            eng.sem_inc(passed, 1)

        def live(j, lag, n):
            return not isinstance(j, int) or 0 <= j - lag < n

        def late(j, k):
            return not isinstance(j, int) or j - k >= 0

        def stage_a(step):
            for j in range(-2, STEPS + 2):
                step(j)

        def group(n):
            return 0 <= n < STEPS

        UH_BANK = (2, 0, 1, 2)

        def messages_of(g):
            return bank[3 + g // 3][:, g % 3 * (D + 1):(g % 3 + 1) * (D + 1)]

        B_FIRST = RING
        B_LAST = B_FIRST + (TILES - 3 - B_FIRST) // RING * RING

        def near(t, th, q, k):
            return t + k, th + (q + k) // RING, (q + k) % RING

        def stage_b(eng, step, last, rebase=None):
            for t in range(B_FIRST):
                step(t, t // RING, t % RING)
            with eng.Fori(B_FIRST // RING, B_LAST // RING) as i:
                if rebase:
                    rebase(i)
                for q in range(RING):
                    step(RING * i + q, i, q)
            if rebase:
                rebase(B_LAST // RING)
            for t in range(B_LAST, last):
                step(t, t // RING, t % RING)

        def pad_tails(eng, first, last):
            eng.wait_ge(fill_ready, 1)
            for p in range(first, last, 4):
                ends = nc.values_load_multi_w_load_instructions(
                    fill[0:1, p:p + 4], engines=[eng.engine], min_val=0, max_val=PAD_SEG - P,
                    skip_runtime_bounds_check_because="a segment holds all tokens and a tile more")[1]
                for at in ends:
                    eng.dma_start(rows[bass.ds(at, P), :], padrow[:, :]).then_inc(padded, 16)

        def load_experts(eng, t, n):
            return nc.values_load_multi_w_load_instructions(
                experts[0:1, bass.ds(t, 1), 0:n].rearrange("o t f -> o (t f)"), engines=[eng.engine], min_val=0,
                max_val=E - 1, skip_runtime_bounds_check_because="an expert's index times 0 or 1")[1]

        @block.sync
        def _(sp):
            for n in range(STEPS):
                if n >= 3:
                    sp.wait_ge(x2_ready, 2 * (n - 2))
                sp.dma_start(X[:, n % 3], x[n * G:(n + 1) * G].rearrange("g n f -> n g f"))\
                    .then_inc(x_in[n % 3], 16)
                if n >= 2:
                    sp.wait_ge(adj_f32, n - 1)
                sp.dma_start(ADJ[:, n % 2], adj[n * G:(n + 1) * G].rearrange("g n f -> n g f"))\
                    .then_inc(adj_in[n % 2], 16)

            sp.wait_ge(consts, N_CONSTS)
            sp.dma_start(rows[PAD_SEG:PAD_SEG + P, :], padrow[:, :]).then_inc(padded, 16)
            pad_tails(sp, 0, NP // 2 // 4 * 4)
            for r in range(4):
                sp.wait_ge(scattered[r], 16 * G * len(range(r, STEPS, 4)))
            sp.wait_ge(padded, 16 * (NP + 1))
            sp.wait_ge(tab_ready, 7)

            def load_rows(t, th, q):
                if live(t, 0, TILES):
                    at = nc.values_load(tile_row[0:1, bass.ds(t, 1)], engines=[sp.engine], min_val=0, max_val=PAD_SEG,
                                        skip_runtime_bounds_check_because="a segment's row or that of the padding")
                    if late(t, RING):
                        wait_alone(sp, stored[q], 16 * th)
                    sp.dma_start(R[:, q], rows[bass.ds(at, P), :]).then_inc(r_in[q], 16)

            stage_b(sp, load_rows, TILES)
            for q in range(RING):
                sp.wait_ge(stored[q], 16 * len(range(q, TILES, RING)))

        @block.gpsimd
        def _(pool):
            n = [0]

            def const(instruction):
                instruction.then_inc(consts, 1)
                n[0] += 1

            def settle():
                pool.wait_ge(consts, n[0])

            const(pool.memset(ident[:], 0.0))
            const(pool.memset(nhalf[:], -0.5))
            const(pool.iota(tcol[:], pattern=[[0, 1]], base=0, channel_multiplier=1,
                            allow_small_or_imprecise_dtypes=True))
            const(pool.memset(ones_b[:], 1.0))
            const(pool.memset(UH[:, :, 2 * D:], 1.0))
            settle()
            const(pool.affine_select(out=ident[:], in_=ident[:], compare_op=ALU.not_equal, fill=1.0, base=0,
                                     pattern=[[-1, P]], channel_multiplier=1))
            assert n[0] == N_EARLY, n[0]

            def deviations(n):
                pool.wait_ge(ve1_ready, 2 * (n + 1))
                if n >= 1:
                    pool.wait_ge(xn_ready, G * n)
                pool.tensor_tensor(r1[:], ve1[:], nhalf[:, 0:G], ALU.pow).then_inc(r1_ready, 1)
                pool.wait_ge(r1_ready, 2 * n + 1)
                pool.tensor_tensor(nm1[:, 1], nm1[:, 0], r1[:], ALU.mult).then_inc(r1_ready, 1)

            deviations(0)
            const(pool.memset(tri[:], 1.0))
            const(pool.memset(padrow[:], 0.0))
            const(pool.memset(carry[:], 0.0))
            const(pool.memset(SR[:, :, :, D:], 0.0))
            const(pool.memset(b2t[:], 0.0))
            const(pool.memset(ones2[:], 0.0))
            const(pool.memset(amax[:], 0.0))
            settle()
            const(pool.affine_select(out=tri[:], in_=tri[:], compare_op=ALU.is_ge, fill=0.0, base=-1,
                                     pattern=[[1, P]], channel_multiplier=-1))
            const(pool.iota(rev[:], pattern=[[0, G], [-1, E]], base=E, channel_multiplier=0,
                            allow_small_or_imprecise_dtypes=True))
            off = 0
            for a in range(E - 1):
                k = E - 1 - a
                const(pool.iota(keys[:, :, off:off + k], pattern=[[0, G], [-1, k]],
                                base=E * (E - a) + E - (a + 1), channel_multiplier=0,
                                allow_small_or_imprecise_dtypes=True))
                const(pool.iota(exp_a[:, off:off + k], pattern=[[0, k]], base=a, channel_multiplier=0,
                                allow_small_or_imprecise_dtypes=True))
                const(pool.iota(exp_b[:, off:off + k], pattern=[[1, k]], base=a + 1, channel_multiplier=0,
                                allow_small_or_imprecise_dtypes=True))
                off += k
            const(pool.iota(rowb[:], pattern=[[0, G], [SEG, NP]], base=0, channel_multiplier=0,
                            allow_small_or_imprecise_dtypes=True))
            const(pool.iota(halfsel[:], pattern=[[0, 1]], base=0, channel_multiplier=1,
                            allow_small_or_imprecise_dtypes=True))
            const(pool.iota(tok[:], pattern=[[P, G]], base=0, channel_multiplier=1,
                            allow_small_or_imprecise_dtypes=True))
            const(pool.iota(padrow[:, TOK:TOK + 1].bitcast(I32), pattern=[[0, 1]], base=TOKENS,
                            channel_multiplier=0))
            assert n[0] == N_CONSTS, n[0]

            def scatter(n, graphs):
                if graphs[0] == 0:
                    pool.wait_ge(pos_ready, n + 1)
                for g in graphs:
                    pool.indirect_dma_start(rows[:, :], bass.IndirectOffsetOnAxis(ap=pos[:, n % 2, g:g + 1], axis=0),
                                            SR[:, n % 4, g, :], None).then_inc(scattered[n % 4], 16)

            def step(j):
                if group(j):
                    pool.wait_ge(ve2_ready, 3 * (j + 1))
                    if j >= 1:
                        pool.wait_ge(r2_used, j)
                        pool.wait_ge(xt_ready, G * j)
                    pool.tensor_tensor(r2[:, 0], ve2[:, 0], nhalf[:, 0:G], ALU.pow).then_inc(r2_ready, 1)
                    pool.wait_ge(r2_ready, 3 * j + 1)
                    pool.tensor_tensor(nm2[:, 1], nm2[:, 0], r2[:, 0], ALU.mult).then_inc(r2_ready, 1)
                    pool.tensor_tensor(r2[:, 1], ve2[:, 1], nhalf[:, 0:G], ALU.pow).then_inc(r2_ready, 1)
                if group(j - 2):
                    scatter(j - 2, range(HG))
                if group(j + 2) and j + 2 > 0:
                    deviations(j + 2)
                if group(j - 2):
                    scatter(j - 2, range(HG, G))
                if j == 0:
                    pool.wait_ge(amax_in, 1)
                    pool.partition_all_reduce(amax_all[:], amax[:], P, RMAX).then_inc(amax_out, 1)

            stage_a(step)

            def normal(t, th, q):
                wait_alone(pool, r_in[q], 16 * (th + 1))
                if late(t, 2):
                    wait_alone(pool, xtb_done, t - 1)
                pool.tensor_scalar(xs[:, q % 2], R[:, q, 0:D], R[:, q, MU:MU + 1], R[:, q, RS:RS + 1], ALU.subtract,
                                   ALU.mult).then_inc(xs_ready, 1)

            def store(t, th, q):
                wait_alone(pool, o_ready, t + 1)
                pool.indirect_dma_start(
                    out[:, :], bass.IndirectOffsetOnAxis(ap=R[:, q, TOK:TOK + 1].bitcast(I32), axis=0),
                    o[:, q, :], None, bounds_check=TOKENS - 1, oob_is_err=False).then_inc(stored[q], 16)

            def tile(t, th, q):
                if isinstance(t, int) and t == 0:
                    for s in range(3):
                        normal(s, 0, s)
                if live(t, -3, TILES):
                    normal(*near(t, th, q, 3))
                if live(t, 2, TILES):
                    store(*near(t, th, q, -2))

            stage_b(pool, tile, TILES + 2)

        @block.scalar
        def _(act):
            act.dma_start(wgnn[:, 0:D], W_upd).then_inc(gnn_w, 16)
            act.dma_start(wgnn[:, D:], W_msg).then_inc(gnn_w, 16)
            act.dma_start(b2s[:], b2).then_inc(gnn_w, 16)
            for g in range(2):
                act.dma_start(bias_rows[:, g, :], bias.rearrange("(o d) -> o d", o=1).partition_broadcast(3))\
                    .then_inc(gnn_w, 16)
            act.dma_start(wr[:], Wr).then_inc(gnn_w, 16)
            act.dma_start(brb[:], br.rearrange("(o e) -> o e", o=1).partition_broadcast(P)).then_inc(gnn_w, 16)
            act.dma_start(b2row[:], b2.rearrange("(o e) d -> o e d", o=1).partition_broadcast(2)).then_inc(gnn_w, 16)
            act.wait_ge(consts, N_EARLY)
            nc.scalar.activation(warm[:], nhalf[:, 0:1], ACT.Exp)
            act.dma_start(small_rows[0:E, :], ln_g).then_inc(ffn_w, 16)
            act.dma_start(small_rows[E:2 * E, :], ln_b).then_inc(ffn_w, 16)
            act.dma_start(small_rows[2 * E:, :], b1.rearrange("e (c p) -> (e c) p", p=P)).then_inc(ffn_w, 16)
            act.dma_start(w1f[:], W1.rearrange("e d h -> d e h")).then_inc(ffn_w, 16)
            for e in range(2):
                act.dma_start(w2f[:, e * 4:(e + 1) * 4], W2[e * 4:(e + 1) * 4].rearrange("e (c p) d -> p e c d", p=P))\
                    .then_inc(ffn_w, 16)

            def step(j):
                m = j + 1
                if group(m):
                    for h in range(2):
                        act.wait_ge(xnt_done, 2 * m + h + 1)
                        nc.scalar.activation(XNT[:, h], bank[h][:], ACT.Copy).then_inc(xnt_ready, 1)
                for k in range(2 * (j - 1), min(2 * j, E + 2 * C)) if j >= 1 else ():
                    c = k % C
                    if k == 0:
                        act.wait_ge(scales_ready, 1)
                    if k < E:
                        nc.scalar.activation(w1f[:, k], w1f[:, k], ACT.Copy, scale=gsc[:, k:k + 1])\
                            .then_inc(w1_scaled, 1)
                    elif k < E + C:
                        nc.scalar.activation(w2h[c][:], w2f[:, :, c], ACT.Copy, scale=sc[:, 4:5])\
                            .then_inc(high_ready, 1)
                    else:
                        act.wait_ge(w1_scaled, E)
                        nc.scalar.activation(w1h[c][:], w1f[:, :, c * P:(c + 1) * P], ACT.Copy).then_inc(high_ready, 1)
                if group(m):
                    for k in range(4):
                        act.wait_ge(uh_done, 4 * m + k + 1)
                        if m >= 1:
                            act.wait_ge(msg_used, G * m)
                        nc.scalar.activation(UH[:, 2 * k:2 * k + 2, 0:2 * D],
                                             bank[UH_BANK[k]][:].rearrange("p (g d) -> p g d", g=2), ACT.Copy)\
                            .then_inc(uh_ready, 1)
                if group(j + 2):
                    n = j + 2
                    act.wait_ge(adj_in[n % 2], 16 * (n // 2 + 1))
                    if n >= 2:
                        act.wait_ge(msg_done, 3 * (n - 1))
                    nc.scalar.activation(AF[:, n % 2], ADJ[:, n % 2], ACT.Copy).then_inc(adj_f32, 1)
                if group(j):
                    act.wait_ge(r2_ready, 3 * j + 2)
                    if j >= 1:
                        act.wait_ge(xt_done, 2 * j)
                    for g in range(G):
                        nc.scalar.activation(XT[:, g], SR[:, j % 4, g, 0:D], ACT.Identity, bias=nm2[:, 1, g:g + 1],
                                             scale=r2[:, 0, g:g + 1]).then_inc(xt_ready, 1)
                if group(j - 1):
                    act.wait_ge(gap_ready, j)
                    nc.scalar.activation(rt[:, 7], rt[:, 6], ACT.Exp).then_inc(ex_ready, 1)
                if group(j):
                    for h in range(2):
                        act.wait_ge(xt_done, 2 * j + h + 1)
                        nc.scalar.activation(XTT[:, h], bank[h][:], ACT.Copy).then_inc(xtt_ready, 1)
                if group(j + 2):
                    act.wait_ge(r1_ready, 2 * (n + 1))
                    if n >= 2:
                        act.wait_ge(xnt_done, 2 * (n - 1))
                    for g in range(G):
                        nc.scalar.activation(XN[:, n % 2, g], X[:, n % 3, g], ACT.Identity, bias=nm1[:, 1, g:g + 1],
                                             scale=r1[:, g:g + 1]).then_inc(xn_ready, 1)
            stage_a(step)
            nc.scalar.activation(warm[:], nhalf[:, 0:1], ACT.Gelu)
            pad_tails(act, NP // 2 // 4 * 4, NP)

            def tile(t, th, q):
                def high(t, q):
                    act.wait_ge(xtb_done, t + 1)
                    nc.scalar.activation(xh[:, q], bank[6 + q % 2][:, 0:P], ACT.Copy).then_inc(xh_ready, 1)

                def gelu(t, q, k, ex):
                    u = 2 * t + k
                    z = 2 * (q % 2) + k
                    wait_alone(act, z_done, u + 1)
                    for c in range(C):
                        nc.scalar.activation(gl[:, z, c * P:(c + 1) * P], bank[z][:, c * P:(c + 1) * P], ACT.Gelu,
                                             bias=b1c[c][:, bass.ds(ex, 1)], scale=sc[:, 2:3])\
                            .then_inc(g_ready, 1)

                if isinstance(t, int) and t == 0:
                    act.wait_ge(weights_ready, 1 + 2 * C)
                    act.wait_ge(tab_ready, 7)
                    high(0, 0)
                if live(t, -1, TILES):
                    high(t + 1, (q + 1) % RING)
                if live(t, 0, TILES):
                    ex = load_experts(act, t, 2)
                    for c in range(C):
                        for k in range(2):
                            act.lower_ap(b1c[c][:, bass.ds(ex[k], 1)])
                    gelu(t, q, 0, ex[0])
                if live(t, 0, TILES):
                    gelu(t, q, 1, ex[1])

            stage_b(act, tile, TILES)

        @block.tensor
        def _(pe):
            mm = nc.tensor.matmul
            pe.wait_ge(consts, N_EARLY)

            def small_columns():
                ns = 2 * E + E * C
                pe.wait_ge(ffn_w, 16 * N_FFN_W)
                nc.tensor.transpose(bank[7][:, 0:ns], small_rows[:, :], ident[0:ns, 0:ns]).then_inc(setup_pe, 1)

            def beta_products():
                pe.wait_ge(cols_ready, 1)
                for e in range(E):
                    for c in range(C):
                        mm(bank[7][:, c * E + e:c * E + e + 1], w1f[:, e, c * P:(c + 1) * P],
                           small_cols[:, E + e:E + e + 1], start=True, stop=True).then_inc(setup_pe, 1)

            def messages(m):
                if m >= 1:
                    pe.wait_ge(uh_ready, 4 * m)
                for h in range(2):
                    pe.wait_ge(xn_ready, G * m + HG * (h + 1))
                    for g in range(HG):
                        last = nc.tensor.transpose(bank[h][:, g * P:(g + 1) * P], XN[:, m % 2, h * HG + g, :], ident[:])
                    last.then_inc(xnt_done, 1)
                if m == 0:
                    pe.wait_ge(gnn_w, 16 * N_GNN_W)
                    pe.wait_ge(bias_ready, 1)
                for k in range(4):
                    pe.wait_ge(xnt_ready, 2 * m + k // 2 + 1)
                    if k == 3:
                        pe.wait_ge(uh_ready, 4 * m + 1)
                    to = bank[UH_BANK[k]]
                    for g in range(2):
                        at = (2 * k + g) % HG * P
                        mm(to[:, g * 2 * D:(g + 1) * 2 * D], XNT[:, k // 2, at:at + P], wgnn[:], start=(g == 0),
                           stop=False)
                    mm(to[:].rearrange("p (g d) -> p g d", g=2)[:, :, 0:D], ones_b[0:3, :], bias3[:], start=False,
                       stop=True).then_inc(uh_done, 1)
                pe.wait_ge(adj_f32, m + 1)
                if m >= 1:
                    pe.wait_ge(msg_used, G * m)
                for g in range(G):
                    pe.wait_ge(uh_ready, 4 * m + g // 2 + 1)
                    last = mm(messages_of(g), AF[:, m % 2, g, :], UH[:, g, D:], start=True, stop=True)
                    if g % 3 == 2 or g == G - 1:
                        last.then_inc(msg_done, 1)

            def logits(j):
                for h in range(2):
                    pe.wait_ge(xt_ready, G * j + HG * (h + 1))
                    if h == 0:
                        pe.wait_ge(uh_ready, 4 * min(j + 2, STEPS))
                        if j == STEPS - 1:
                            pe.wait_ge(xtt_ready, 2 * j)
                    for g in range(HG):
                        last = nc.tensor.transpose(bank[h][:, g * P:(g + 1) * P], XT[:, h * HG + g, :], ident[:])
                    last.then_inc(xt_done, 1)
                for h in range(2):
                    pe.wait_ge(xtt_ready, 2 * j + h + 1)
                    if j >= 1:
                        pe.wait_ge(lg_used, j)
                    for g in range(HG):
                        gg = h * HG + g
                        last = mm(bank[6][:, gg * E:(gg + 1) * E], XTT[:, h, g * P:(g + 1) * P], wr[:],
                                  start=True, stop=True)
                    last.then_inc(lg_done, 1)

            def ranks(n):
                pe.wait_ge(oh_ready, n + 1)
                if n >= 1:
                    pe.wait_ge(pos_ready, n)
                mm(bank[7][:, 0:G * NP], tri[:], oh[:].rearrange("p g n -> p (g n)"), start=True, stop=False)
                for k in range(1, G):
                    mm(bank[7][:, k * NP:G * NP], ones_b[:], oh[:, 0:G - k].rearrange("p g n -> p (g n)"),
                       start=False, stop=False)
                mm(bank[7][:, 0:G * NP].rearrange("p (g n) -> p g n", g=G), ones_b[:],
                   carry[:].unsqueeze(1).to_broadcast([P, G, NP]), start=False, stop=True).then_inc(rank_done, 1)

            def totals():
                pe.wait_ge(oh_ready, STEPS)
                pe.wait_ge(lg_used, STEPS)
                for g in range(G):
                    mm(bank[6][:, 0:NP], ones_b[:], oh[:, g], start=(g == 0), stop=False)
                mm(bank[6][:, 0:NP], ones_b[:], carry[:], start=False, stop=True).then_inc(total_done, 1)

            def step(j):
                if j == STEPS + 1:
                    totals()
                if group(j - 2):
                    ranks(j - 2)
                if group(j - 1):
                    logits(j - 1)
                if group(j + 1):
                    messages(j + 1)
                if j == -1:
                    small_columns()
                if j == 0:
                    beta_products()

            stage_a(step)
            pe.wait_ge(fld_ready, 1)
            for f in range(3):
                mm(bank[5][0:1, f * P:(f + 1) * P], fld[:, f:f + 1], ident[:], start=True, stop=True)\
                    .then_inc(fld_row, 1)

            pe.wait_ge(weights_ready, 1 + 2 * C)
            pe.wait_ge(tab_ready, 7)

            def turn(t, q):
                pe.wait_ge(xs_ready, t + 1)
                nc.tensor.transpose(bank[6 + q % 2][:, 0:P], xs[:, q % 2, :], ident[:]).then_inc(xtb_done, 1)

            def up(t, q, k, ex):
                z = 2 * (q % 2) + k
                if k == 0:
                    pe.wait_ge(xl_ready, t + 1)
                for c in range(C):
                    zz = bank[z][:, c * P:(c + 1) * P]
                    wh = w1h[c][:, bass.ds(ex, 1), :]
                    mm(zz, wh, xh[:, q], start=True, stop=False)
                    mm(zz, wh, xl[:, q], start=False, stop=False)
                    last = mm(zz, w1l[c][:, bass.ds(ex, 1), :], xh[:, q], start=False, stop=True)
                last.then_inc(z_done, 1)

            def down(t, q, k, ex):
                u, z = 2 * t + k, 2 * (q % 2) + k
                pe.wait_ge(h_ready, 2 * (u + 1))
                y = bank[4 + q % 2][:, k * D:(k + 1) * D]
                mm(y, ones2[:], b2t[:, bass.ds(ex, 1), :], start=True, stop=False)
                for c in range(C):
                    mm(y, hh[:, z, c * P:(c + 1) * P], w2h[c][:, bass.ds(ex, 1), :], start=False, stop=False)
                    mm(y, hh[:, z, c * P:(c + 1) * P], w2l[c][:, bass.ds(ex, 1), :], start=False, stop=False)
                    last = mm(y, hl[:, z, c * P:(c + 1) * P], w2h[c][:, bass.ds(ex, 1), :], start=False,
                              stop=(c == C - 1))
                last.then_inc(y_done, 1)

            def addresses_up(ex):
                for c in range(C):
                    for w in (w1h, w1l):
                        pe.lower_ap(w[c][:, bass.ds(ex, 1), :], for_matmul_weights=True)

            def addresses_down(ex):
                pe.lower_ap(b2t[:, bass.ds(ex, 1), :])
                for c in range(C):
                    for w in (w2h, w2l):
                        pe.lower_ap(w[c][:, bass.ds(ex, 1), :])

            def tile(t, th, q):
                if isinstance(t, int) and t == 0:
                    turn(0, 0)
                    turn(1, 1)
                ex = load_experts(pe, t, 4)
                if live(t, 0, TILES):
                    addresses_up(ex[0])
                    up(t, q, 0, ex[0])
                if live(t, 2, TILES):
                    addresses_down(ex[2])
                    down(t - 2, (q - 2) % RING, 1, ex[2])
                if live(t, 0, TILES):
                    addresses_up(ex[1])
                    up(t, q, 1, ex[1])
                if live(t, 1, TILES):
                    addresses_down(ex[3])
                    down(t - 1, (q - 1) % RING, 0, ex[3])
                if live(t, -2, TILES):
                    turn(t + 2, (q + 2) % RING)

            stage_b(pe, tile, TILES + 2)

        @block.vector
        def _(v):
            ts, tt, stt = nc.vector.tensor_scalar, nc.vector.tensor_tensor, nc.vector.scalar_tensor_tensor
            done = Done(v, dve)

            def bias_parts():
                v.wait_ge(consts, N_EARLY)
                for k in range(3):
                    done(ts(sel3[:, k:k + 1], tcol[0:3, :], float(k), None, ALU.is_equal))
                v.wait_ge(gnn_w, 16 * N_GNN_W)
                rest = bias_rows
                for k in range(3):
                    m = done(nc.vector.tensor_copy(bias_part[:, k], rest[:]))
                    done.wait(m)
                    if k < 2:
                        m = done(tt(bias_rest[:], rest[:], bias_part[:, k], ALU.subtract))
                        rest = bias_rest
                        done.wait(m)
                m = done(ts(bias3[:], bias_part[:, 0], sel3[:, 0:1], None, ALU.mult))
                done.wait(m)
                m = done(stt(bias3[:], bias_part[:, 1], sel3[:, 1:2], bias3[:], ALU.mult, ALU.add))
                done.wait(m)
                stt(bias3[:], bias_part[:, 2], sel3[:, 2:3], bias3[:], ALU.mult, ALU.add).then_inc(bias_ready, 1)

            def columns():
                v.wait_ge(setup_pe, 1)
                nc.vector.tensor_copy(small_cols[:], bank[7][:, 0:2 * E + E * C]).then_inc(cols_ready, 1)

            def scales():
                v.wait_ge(ffn_w, 16 * N_FFN_W)
                v.wait_ge(gnn_w, 16 * N_GNN_W)
                m = done(nc.vector.tensor_reduce(amw[:], w1f[:], AX.X, ALU.max, apply_absolute_value=True))
                done(nc.vector.tensor_reduce(amax[:, 1:2], w2f[:].rearrange("p e c d -> p (e c d)"), AX.X, ALU.max,
                                             apply_absolute_value=True))
                done(nc.vector.tensor_reduce(amax[0:E, 3:4], b2s[:], AX.X, ALU.max, apply_absolute_value=True))
                done.wait(m)
                v.wait_ge(cols_ready, 1)
                m = done(tt(amw[:], amw[:], small_cols[:, 0:E], ALU.mult))
                v.wait_ge(setup_pe, 1 + E * C)
                mb = done(tt(b1s[:], bank[7][:, 0:E * C].rearrange("p (c e) -> p c e", c=C),
                             small_cols[:, 2 * E:].rearrange("p (e c) -> p c e", c=C), ALU.add))
                done.wait(mb)
                for c in range(C):
                    done(nc.vector.tensor_copy(b1c[c][:], b1s[:, c]))
                done(nc.vector.tensor_reduce(amax[:, 2:3], b1s[:].rearrange("p c e -> p (c e)"), AX.X, ALU.max,
                                             apply_absolute_value=True))
                nc.vector.tensor_reduce(amax[:, 0:1], amw[:], AX.X, ALU.max, apply_absolute_value=True)\
                    .then_inc(amax_in, 1)
                v.wait_ge(amax_out, 1)
                m = done(ts(sc[:, 0:1], amax_all[:, 0:1], 1e-30, None, ALU.max))
                m = done(tt(sc[:, 1:2], amax_all[:, 1:2], amax_all[:, 3:4], ALU.max))
                done.wait(m)
                done(ts(sc[:, 1:2], sc[:, 1:2], 1e-30, None, ALU.max))
                m = done(stt(sc[:, 7:8], sc[:, 0:1], float(D), amax_all[:, 2:3], ALU.mult, ALU.add))
                done.wait(m)
                m = done(ts(sc[:, 8:9], sc[:, 7:8], 1.0, None, ALU.max))
                done.wait(m)
                done(ts(sc[:, 9:10].bitcast(I32), sc[:, 0:1].bitcast(I32), 0x7F800000, None, ALU.bitwise_and))
                done(ts(sc[:, 10:11].bitcast(I32), sc[:, 1:2].bitcast(I32), 0x7F800000, None, ALU.bitwise_and))
                m = done(ts(sc[:, 11:12].bitcast(I32), sc[:, 8:9].bitcast(I32), 0x7F800000, None, ALU.bitwise_and))
                done.wait(m)
                m = done(nc.vector.reciprocal(sc[:, 12:15], sc[:, 9:12]))
                done.wait(m)
                done(ts(sc[:, 2:3], sc[:, 9:10], 2.0 ** -9, None, ALU.mult))
                done(ts(sc[:, 3:4], sc[:, 12:13], 2.0 ** 9, None, ALU.mult))
                done(ts(sc[:, 4:5], sc[:, 13:14], 2.0 ** 9, None, ALU.mult))
                done(ts(sc[:, 5:6], sc[:, 14:15], 2.0 ** 14, None, ALU.mult))
                m = done(tt(sc[:, 6:7], sc[:, 10:11], sc[:, 11:12], ALU.mult))
                done.wait(m)
                done(ts(sc[:, 6:7], sc[:, 6:7], 2.0 ** -23, None, ALU.mult))
                ts(gsc[:], small_cols[:, 0:E], sc[:, 3:4], None, ALU.mult).then_inc(scales_ready, 1)

            def b2_rows():
                done(ts(b2sc[:], b2row[:], sc[0:2, 4:5], None, ALU.mult))
                m = done(ts(ones2[0:2, :], ident[0:2, :], 0.0, sc[0:2, 5:6], ALU.mult, ALU.add))
                done.wait(m)
                m = done(nc.vector.tensor_copy(b2hi[:], b2sc[:]))
                done.wait(m)
                m = done(tt(b2hi32[:], b2sc[:], b2hi[:], ALU.subtract))
                done.wait(m)
                m = done(tt(b2hi32[:], b2hi32[:], b2hi[:], ALU.subtract))
                done.wait(m)
                stt(b2t[0:2].rearrange("p e d -> p (e d)"), b2hi32[:].rearrange("p e d -> p (e d)"), halfsel[:, 0:1],
                    b2hi[:].rearrange("p e d -> p (e d)"), ALU.mult, ALU.add)\
                    .then_inc(weights_ready, 1)

            def low_halves(c):
                v.wait_ge(high_ready, C + c + 1)
                tt(w1l[c][:], w1f[:, :, c * P:(c + 1) * P], w1h[c][:], ALU.subtract).then_inc(weights_ready, 1)
                stt(w2l[c][:], w2f[:, :, c], sc[:, 4:5], w2h[c][:], ALU.mult, ALU.subtract)\
                    .then_inc(weights_ready, 1)

            l, q1, o1_, q2 = (L[:, i] for i in range(4))
            m1, k1, m2, k2, hi, key, gap, ex, den, w1_, w2_, sw, dw, sdw, lo = (rt[:, i] for i in range(15))
            shape = [P, G, E]

            def wide(a):
                return a.unsqueeze(2).to_broadcast(shape)

            class Statistics:

                def __init__(self, rows_of, st, mv):
                    self.rows_of, self.st, self.mv, self.marks = rows_of, st, mv, []

                def one(self):
                    k = len(self.marks)
                    if k < G:
                        self.marks.append(done(nc.vector.bn_stats(self.st[:, k], self.rows_of(k))))
                    elif k < 2 * G:
                        done.wait(self.marks[k - G])
                        self.marks.append(done(nc.vector.bn_aggr(self.mv[:, k - G], self.st[:, k - G])))

                def rest(self):
                    while len(self.marks) < 2 * G:
                        self.one()
                    return self.marks[-1]

            def residual(j):
                for b in range(3):
                    n = min(3, G - 3 * b)
                    v.wait_ge(msg_done, 3 * j + b + 1)
                    m = done(nc.vector.tensor_copy(
                        dg[:, 3, 3 * b:3 * b + n],
                        bank[3 + b][:, 0:n * (D + 1)].rearrange("p (g d) -> p g d", g=n)[:, :, D]))
                done.wait(m)
                m = done(ts(dg[:, 0], dg[:, 3], 1.0, None, ALU.max))
                done.wait(m)
                m = done(nc.vector.reciprocal(dg[:, 1], dg[:, 0]))
                done.wait(m)
                stt(dg[:, 2], dg[:, 3], 0.0, dg[:, 1], ALU.is_gt, ALU.mult).then_inc(deg_ready, 1)
                v.wait_ge(deg_ready, j + 1)
                for g in range(G):
                    stt(T[:, g // HG, g % HG], messages_of(g)[:, 0:D], dg[:, 2, g:g + 1], UH[:, g, 0:D],
                        ALU.mult, ALU.add).then_inc(msg_used, 1)
                if j >= 4:
                    v.wait_ge(scattered[j % 4], 16 * G * (j // 4))
                for h in range(2):
                    v.wait_ge(msg_used, HG * (2 * j + h + 1))
                    stt(SR[:, j % 4, h * HG:(h + 1) * HG, 0:D], T[:, h], 0.0, X[:, j % 3, h * HG:(h + 1) * HG],
                        ALU.max, ALU.add).then_inc(x2_ready, 1)
                v.wait_ge(x2_ready, 2 * (j + 1))

            def places(n, stats):
                v.wait_ge(ex_ready, n + 1)
                m = done(ts(den, ex, 1.0, None, ALU.add))
                stats.one()
                v.wait_ge(rank_done, n + 1)
                with nc.allow_low_precision(reason="whole numbers of at most 256"):
                    mc = done(nc.vector.tensor_reduce(csum[:], oh[:].rearrange("p g n -> p n g"), AX.X, ALU.add))
                mr = done(tt(rk[:], bank[7][:, 0:G * NP].rearrange("p (g n) -> p g n", g=G), rowb[:], ALU.add))
                done.wait(m)
                m = done(nc.vector.reciprocal(w1_, den))
                stats.one()
                done.wait(mc)
                done(tt(carry[:], carry[:], csum[:], ALU.add))
                done.wait(mr)
                mr = done(tt(rk[:], rk[:], oh[:], ALU.mult))
                done.wait(m)
                m = done(ts(w1_, w1_, sc[:, 6:7], None, ALU.mult))
                stats.one()
                done.wait(m)
                m = done(tt(w2_, ex, w1_, ALU.mult))
                stats.one()
                done.wait(m)
                m = done(tt(dw, w2_, w1_, ALU.subtract))
                done(nc.vector.tensor_copy(SR[:, n % 4, :, TOK].bitcast(I32), tok[:]))
                stats.one()
                done.wait(m)
                m = done(tt(sdw, sw, dw, ALU.mult))
                mt = done(ts(tok[:], tok[:], float(G * N), None, ALU.add))
                stats.one()
                done.wait(m)
                done(tt(SR[:, n % 4, :, WA], w1_, sdw, ALU.add))
                done(tt(SR[:, n % 4, :, WB], w2_, sdw, ALU.subtract))
                done.wait(mr)
                if n >= 2:
                    v.wait_ge(scattered[(n - 2) % 4], 16 * G * ((n - 2) // 4 + 1))
                with nc.allow_low_precision(reason="sums of whole numbers below 2**24"):
                    nc.vector.tensor_reduce(pos[:, n % 2], rk[:], AX.X, ALU.add).then_inc(pos_ready, 1)

            def route(n, stats):
                v.wait_ge(lg_done, 2 * (n + 1))
                tt(l, bank[6][:, 0:G * E].rearrange("p (g e) -> p g e", g=G),
                   brb[:].unsqueeze(1).to_broadcast(shape), ALU.add).then_inc(lg_used, 1)
                stats.one()
                v.wait_ge(lg_used, n + 1)
                m = done(nc.vector.tensor_reduce(m1, l, AX.X, ALU.max))
                stats.one()
                done.wait(m)
                m = done(tt(q1, l, wide(m1), ALU.is_equal))
                stats.one()
                done.wait(m)
                m = done(tt(q1, q1, rev[:], ALU.mult))
                stats.one()
                done.wait(m)
                m = done(nc.vector.tensor_reduce(k1, q1, AX.X, ALU.max))
                stats.one()
                done.wait(m)
                m = done(tt(o1_, rev[:], wide(k1), ALU.is_equal))
                stats.one()
                done.wait(m)
                m = done(stt(q2, o1_, BIG, l, ALU.mult, ALU.add))
                stats.one()
                done.wait(m)
                m = done(nc.vector.tensor_reduce(m2, q2, AX.X, ALU.max))
                stats.one()
                done.wait(m)
                m = done(tt(q1, q2, wide(m2), ALU.is_equal))
                tt(gap, m2, m1, ALU.subtract).then_inc(gap_ready, 1)
                stats.one()
                done.wait(m)
                m = done(tt(q1, q1, rev[:], ALU.mult))
                stats.one()
                done.wait(m)
                m = done(nc.vector.tensor_reduce(k2, q1, AX.X, ALU.max))
                stats.one()
                done.wait(m)
                done(tt(lo, k1, k2, ALU.min))
                m = done(tt(hi, k1, k2, ALU.max))
                done(tt(sw, k2, k1, ALU.is_gt))
                done.wait(m)
                m = done(stt(key, hi, float(E), lo, ALU.mult, ALU.add))
                stats.one()
                done.wait(m)
                tt(oh[:], keys[:], key.unsqueeze(2).to_broadcast([P, G, NP]), ALU.is_equal).then_inc(oh_ready, 1)

            def tails():
                v.wait_ge(total_done, 1)
                m = done(nc.vector.tensor_copy(cntf[:], bank[6][:, 0:NP]))
                done(ts(cnti[:], bank[6][:, 0:NP], float(P - 1), None, ALU.add))
                done.wait(m)
                tt(fill[:], cntf[0:1], rowb[0:1, 0], ALU.add).then_inc(fill_ready, 1)

            class Nothing:
                def one(self):
                    pass

            def step(j):
                stats1 = Nothing()
                if group(j):
                    residual(j)
                    stats2 = Statistics(lambda g: SR[:, j % 4, g, 0:D], st2, mv2)
                if group(j):
                    m = stats2.rest()
                    if j >= 1:
                        v.wait_ge(r2_ready, 3 * j)
                    done.wait(m)
                    ts(ve2[:, 0], mv2[:, :, 1], EPS, None, ALU.add).then_inc(ve2_ready, 1)
                    ts(nm2[:, 0], mv2[:, :, 0], -1.0, None, ALU.mult).then_inc(ve2_ready, 1)
                    v.wait_ge(ve2_ready, 3 * j + 1)
                    stt(ve2[:, 1], ve2[:, 0], EPS, mv2[:, :, 1], ALU.mult, ALU.add).then_inc(ve2_ready, 1)
                if group(j + 2):
                    n = j + 2
                    v.wait_ge(x_in[n % 3], 16 * (n // 3 + 1))
                    stats1 = Statistics(lambda g: X[:, n % 3, g], st1, mv1)
                if j == STEPS + 1:
                    tails()
                if group(j - 2):
                    places(j - 2, stats1)
                if group(j - 1):
                    route(j - 1, stats1)
                if group(j + 2):
                    m = stats1.rest()
                    if n >= 1:
                        v.wait_ge(r1_ready, 2 * n)
                    done.wait(m)
                    ts(ve1[:], mv1[:, :, 1], EPS, None, ALU.add).then_inc(ve1_ready, 1)
                    ts(nm1[:, 0], mv1[:, :, 0], -1.0, None, ALU.mult).then_inc(ve1_ready, 1)
                if group(j):
                    done(nc.vector.tensor_copy(SR[:, j % 4, :, MU], mv2[:, :, 0]))
                    v.wait_ge(r2_ready, 3 * (j + 1))
                    nc.vector.tensor_copy(SR[:, j % 4, :, RS], r2[:, 1]).then_inc(r2_used, 1)
                if j == -2:
                    bias_parts()
                if j == -1:
                    v.wait_ge(consts, N_CONSTS)
                    columns()
                if j == 0:
                    scales()
                if STEPS - 1 <= j <= STEPS:
                    low_halves(j - STEPS + 1)

            stage_a(step)

            done(nc.vector.memset(fld[:, 3:4], 0.0))
            m = done(ts(cnti[:], cnti[:], 7, None, ALU.logical_shift_right))
            done.wait(m)
            m = done(nc.vector.tensor_copy(ntf[:], cnti[:]))
            done.wait(m)
            m = done(nc.vector.tensor_copy(inc[:, 0], ntf[:]))
            done.wait(m)
            a, s = 0, 1
            while s < NP:
                done(tt(inc[:, 1 - a, s:], inc[:, a, s:], inc[:, a, :NP - s], ALU.add))
                m = done(nc.vector.tensor_copy(inc[:, 1 - a, :s], inc[:, a, :s]))
                done.wait(m)
                a, s = 1 - a, 2 * s
            last = inc[:, a]
            m = done(tt(tw[:, 0], last, ntf[:], ALU.subtract))
            done.wait(m)
            done(ts(tw[:, 1], tw[:, 0], tcol[:, 0:1], None, ALU.is_le))
            m = done(ts(tw[:, 2], last, tcol[:, 0:1], None, ALU.is_gt))
            done.wait(m)
            m = done(tt(tw[:, 1], tw[:, 1], tw[:, 2], ALU.mult))
            m = done(ts(tw[:, 3], tw[:, 0], tcol[:, 0:1], -float(P), ALU.subtract, ALU.mult))
            done.wait(m)
            m = done(tt(tw[:, 3], tw[:, 3], rowb[:, 0], ALU.add))
            done.wait(m)
            m = done(ts(tw[:, 3], tw[:, 3], float(PAD_SEG), None, ALU.subtract))
            done.wait(m)
            m = done(tt(tw[:, 3], tw[:, 3], tw[:, 1], ALU.mult))
            done(tt(tw[:, 0], exp_a[:], tw[:, 1], ALU.mult))
            m = done(tt(tw[:, 2], exp_b[:], tw[:, 1], ALU.mult))
            done.wait(m)
            done(nc.vector.tensor_reduce(fld[:, 0:1], tw[:, 0], AX.X, ALU.add))
            done(nc.vector.tensor_reduce(fld[:, 1:2], tw[:, 2], AX.X, ALU.add))
            m = done(nc.vector.tensor_reduce(fld[:, 2:3], tw[:, 3], AX.X, ALU.add))
            done.wait(m)
            ts(fld[:, 2:3], fld[:, 2:3], float(PAD_SEG), None, ALU.add).then_inc(fld_ready, 1)
            b2_rows()
            low_halves(2)
            low_halves(3)
            v.wait_ge(fld_row, 3)
            for k in range(2):
                nc.vector.tensor_copy(experts[:, :, k], bank[5][0:1, k * P:(k + 1) * P]).then_inc(tab_ready, 1)
                back = 1 if k == 0 else 2
                nc.vector.tensor_copy(experts[:, back:, 3 - k], bank[5][0:1, k * P:(k + 1) * P - back])\
                    .then_inc(tab_ready, 1)
            nc.vector.memset(experts[:, 0, 3:4], 0).then_inc(tab_ready, 1)
            nc.vector.memset(experts[:, 0:2, 2:3], 0).then_inc(tab_ready, 1)
            nc.vector.tensor_copy(tile_row[:], bank[5][0:1, 2 * P:3 * P]).then_inc(tab_ready, 1)

            def low(t, q):
                v.wait_ge(xh_ready, t + 1)
                tt(xl[:, q], bank[6 + q % 2][:, 0:P], xh[:, q], ALU.subtract).then_inc(xl_ready, 1)

            def high_half(t, q, k):
                u, z = 2 * t + k, 2 * (q % 2) + k
                v.wait_ge(g_ready, C * (u + 1))
                ts(hh[:, z], gl[:, z], sc[:, 5:6], None, ALU.mult).then_inc(h_ready, 1)

            def low_half(t, q, k):
                u, z = 2 * t + k, 2 * (q % 2) + k
                v.wait_ge(h_ready, 2 * u + 1)
                stt(hl[:, z], gl[:, z], sc[:, 5:6], hh[:, z], ALU.mult, ALU.subtract).then_inc(h_ready, 1)

            def combine_a(t, th, q):
                v.wait_ge(y_done, 2 * (t + 1))
                done(stt(o1[:, q % 2], bank[4 + q % 2][:, 0:D], R[:, q, WA:WA + 1], R[:, q, 0:D], ALU.mult,
                         ALU.add))

            def combine_b(t, th, q, a_done):
                done.wait(a_done)
                stt(o[:, q], bank[4 + q % 2][:, D:2 * D], R[:, q, WB:WB + 1], o1[:, q % 2], ALU.mult, ALU.add)\
                    .then_inc(o_ready, 1)

            def tile(t, th, q):
                _, th2, q2 = near(t, th, q, -2)
                if isinstance(t, int) and t == 0:
                    low(0, 0)
                if live(t, 2, TILES):
                    combine_a(t - 2, th2, q2)
                    a_done = done.base + done.n
                if live(t, -1, TILES):
                    low(t + 1, (q + 1) % RING)
                if live(t, 0, TILES):
                    high_half(t, q, 0)
                if live(t, 2, TILES):
                    combine_b(t - 2, th2, q2, a_done)
                if live(t, 0, TILES):
                    low_half(t, q, 0)
                    high_half(t, q, 1)
                    low_half(t, q, 1)

            b0 = [done.base + done.n, 0]

            def rebase_b(i):
                done.rebase(b0[0] + RING * i - 2)

            stage_b(v, tile, TILES + 2, rebase_b)


N_CONSTS = 11 + 3 + 3 * (E - 1) + 5
N_EARLY = 6
RMAX = bass.bass_isa.ReduceOp.max

_INS = ["x", "adj", "L0_gnn_W_msg", "L0_gnn_W_upd", "L0_gnn_bias", "L0_ffn_Wr", "L0_ffn_br", "L0_ffn_ln_g",
        "L0_ffn_ln_b", "L0_ffn_W1", "L0_ffn_b1", "L0_ffn_W2", "L0_ffn_b2"]


def kernel(**inputs):
    import numpy as _np
    import concourse.bacc as _bacc
    from concourse.bass_utils import run_bass_kernel_spmd as _run

    nc = _bacc.Bacc("TRN2", target_bir_lowering=False, num_devices=1)
    arrays, args = {}, []
    for name in _INS:
        a = _np.ascontiguousarray(inputs[name])
        arrays[f"in_{name}"] = a
        args.append(nc.dram_tensor(f"in_{name}", a.shape, mybir.dt.from_np(a.dtype), kind="ExternalInput").ap())
    out = nc.dram_tensor("out_rows", (TOKENS, D), F32, kind="ExternalOutput").ap()
    moe_gnn(nc, *args, out)
    r = _run(nc, [arrays], core_ids=[0])
    return r.results[0]["out_rows"].reshape(B, N, D)
```
